# Optimizing a Trainium2 kernel written in Bass

```python
import numpy as np
import jax
import jax.numpy as jnp

def _softmax(x, axis=-1):
    return jax.nn.softmax(x, axis=axis)

def _gelu(x):
    return jax.nn.gelu(x, approximate=True)

def _silu(x):
    return jax.nn.silu(x)

def _sigmoid(x):
    return jax.nn.sigmoid(x)

def _layernorm(x, axis=-1, eps=1e-05):
    m = jnp.mean(x, axis=axis, keepdims=True)
    v = jnp.var(x, axis=axis, keepdims=True)
    return (x - m) / jnp.sqrt(v + eps)

def _scatter_add(tgt, idx, src, axis=0):
    return tgt.at[idx].add(src)

def _segment_sum(src, seg, n):
    return jax.ops.segment_sum(src, seg, n)
kernel_name = 'mk_seq_preln_d1_jaxref_r8_388b5b'

def setup_inputs(seed: int=0):
    np.random.seed(seed)
    _w = jnp.asarray

    def _L0_attn_setup():
        import jax, jax.numpy as jnp
        import numpy as np
        B, T, D = (4, 512, 128)

        def _rmsnorm(y, w):
            return y * jax.lax.rsqrt(jnp.mean(y * y, axis=-1, keepdims=True) + 1e-06) * w
        key = jax.random.key(seed)
        ks = jax.random.split(key, 6)
        std = np.sqrt(2.0 / D).astype(np.float32)
        return {'x': jax.random.normal(ks[0], (B, T, D), dtype=jnp.float32), 'Wr': jax.random.normal(ks[1], (D, D), dtype=jnp.float32) * std, 'Wk': jax.random.normal(ks[2], (D, D), dtype=jnp.float32) * std, 'Wv': jax.random.normal(ks[3], (D, D), dtype=jnp.float32) * std, 'Wo': jax.random.normal(ks[4], (D, D), dtype=jnp.float32) * std, 'decay': jnp.ones((D,), dtype=jnp.float32) * 0.99, 'ln_w': jnp.ones((D,), dtype=jnp.float32)}
    _L0_attn_in = _L0_attn_setup()

    def _L0_ffn_setup():
        import jax, jax.numpy as jnp
        import numpy as np
        NUM_EXPERTS = 8
        IN_FEATURES = 128
        HIDDEN_FEATURES = 512
        GATE_DIM = 16
        EPS = 0.0001
        key = jax.random.key(seed)
        ks = jax.random.split(key, 7)
        hidden_states = jax.random.normal(ks[0], (1, 256, IN_FEATURES), dtype=jnp.float32)
        wg_red = jax.random.normal(ks[1], (GATE_DIM, IN_FEATURES), dtype=jnp.float32) * 0.02
        wg = jax.random.normal(ks[2], (NUM_EXPERTS, GATE_DIM), dtype=jnp.float32)
        w1 = jax.random.uniform(ks[3], (NUM_EXPERTS, IN_FEATURES, HIDDEN_FEATURES), dtype=jnp.float32)
        b1 = jax.random.uniform(ks[4], (NUM_EXPERTS, HIDDEN_FEATURES), dtype=jnp.float32)
        w2 = jax.random.uniform(ks[5], (NUM_EXPERTS, HIDDEN_FEATURES, IN_FEATURES), dtype=jnp.float32)
        b2 = jax.random.uniform(ks[6], (NUM_EXPERTS, IN_FEATURES), dtype=jnp.float32)
        return {'hidden_states': hidden_states, 'wg_red': wg_red, 'wg': wg, 'w1': w1, 'b1': b1, 'w2': w2, 'b2': b2}
    _L0_ffn_in = _L0_ffn_setup()
    _d = {'L0_attn_x': _L0_attn_in['x'], 'L0_attn_Wr': _L0_attn_in['Wr'], 'L0_attn_Wk': _L0_attn_in['Wk'], 'L0_attn_Wv': _L0_attn_in['Wv'], 'L0_attn_Wo': _L0_attn_in['Wo'], 'L0_attn_decay': _L0_attn_in['decay'], 'L0_attn_ln_w': _L0_attn_in['ln_w'], 'L0_ffn_wg_red': _L0_ffn_in['wg_red'], 'L0_ffn_wg': _L0_ffn_in['wg'], 'L0_ffn_w1': _L0_ffn_in['w1'], 'L0_ffn_b1': _L0_ffn_in['b1'], 'L0_ffn_w2': _L0_ffn_in['w2'], 'L0_ffn_b2': _L0_ffn_in['b2']}
    _x0 = _d['L0_attn_x']
    _d['L0_attn_x'] = jax.random.normal(jax.random.fold_in(jax.random.key(seed), 1), (4, 1024, 128), dtype=_x0.dtype)
    del _x0
    return _d

def reference(L0_attn_x, L0_attn_Wr, L0_attn_Wk, L0_attn_Wv, L0_attn_Wo, L0_attn_decay, L0_attn_ln_w, L0_ffn_wg_red, L0_ffn_wg, L0_ffn_w1, L0_ffn_b1, L0_ffn_w2, L0_ffn_b2):

    def _L0_attn_ref(x, Wr, Wk, Wv, Wo, decay, ln_w):
        import jax, jax.numpy as jnp
        import numpy as np
        B, T, D = (4, 512, 128)

        def _rmsnorm(y, w):
            return y * jax.lax.rsqrt(jnp.mean(y * y, axis=-1, keepdims=True) + 1e-06) * w
        Bsz, Tlen, Dm = x.shape
        r = jax.nn.sigmoid(jnp.einsum('btd,ed->bte', x, Wr))
        k = jnp.einsum('btd,ed->bte', x, Wk)
        v = jnp.einsum('btd,ed->bte', x, Wv)
        dec = jax.nn.sigmoid(decay)
        log_decay = jnp.log(jnp.clip(dec, 1e-07))
        t = jnp.arange(Tlen, dtype=x.dtype)[:, None]
        scale = jnp.exp(t * log_decay[None, :])
        kv = k * v
        cum = jnp.cumsum(kv / jnp.clip(scale, 1e-10)[None], axis=1)
        state = cum * scale[None]
        y = _rmsnorm(r * state, ln_w)
        return jnp.einsum('btd,ed->bte', y, Wo)

    def _L0_ffn_ref(hidden_states, wg_red, wg, w1, b1, w2, b2):
        import jax, jax.numpy as jnp
        import numpy as np
        NUM_EXPERTS = 8
        IN_FEATURES = 128
        HIDDEN_FEATURES = 512
        GATE_DIM = 16
        EPS = 0.0001
        b, t, c = hidden_states.shape
        x = hidden_states.reshape(-1, c)
        xr = x @ wg_red.T
        wg_unit = wg / jnp.maximum(jnp.linalg.norm(wg, axis=1, keepdims=True), EPS)
        logits = xr @ wg_unit.T
        gates = jax.nn.softmax(logits, axis=1)
        indices_s = jnp.argmax(gates, axis=1)
        scores = jnp.max(gates, axis=1)
        E = wg.shape[0]
        out = jnp.zeros_like(x)
        for e in range(E):
            mask = (indices_s == e).astype(x.dtype)[:, None]
            h = jax.nn.gelu(x @ w1[e] + b1[e], approximate=False)
            out = out + mask * (h @ w2[e] + b2[e])
        out = out * scores[:, None]
        return out.reshape(b, t, c)
    x = L0_attn_x
    x = x + _L0_attn_ref(_layernorm(x, axis=-1), L0_attn_Wr, L0_attn_Wk, L0_attn_Wv, L0_attn_Wo, L0_attn_decay, L0_attn_ln_w)
    x = x + _L0_ffn_ref(_layernorm(x, axis=-1), L0_ffn_wg_red, L0_ffn_wg, L0_ffn_w1, L0_ffn_b1, L0_ffn_w2, L0_ffn_b2)
    return x

_drawn_inputs = setup_inputs


def setup_inputs(seed=0):
    import zlib

    import numpy as np

    out = dict(_drawn_inputs(seed))
    spreads = {'L0_attn_decay': (0.9900000095367432, 0.2), 'L0_attn_ln_w': (1.0, 0.6)}
    factors = {'L0_ffn_b1': 8.0, 'L0_ffn_b2': 8.0}
    for name, (base, spread) in spreads.items():
        noise = np.random.default_rng([zlib.crc32(name.encode()), seed]).standard_normal(out[name].shape)
        drawn = base * np.exp(spread * noise) if base else spread * noise
        out[name] = jnp.asarray(drawn.astype(out[name].dtype))
    for name, factor in factors.items():
        out[name] = (out[name] * factor).astype(out[name].dtype)
    return out
```

```python
import concourse.bass as bass
from concourse import mybir
from contextlib import ExitStack

F32 = mybir.dt.float32
BF16 = mybir.dt.bfloat16
I32 = mybir.dt.int32
ALU = mybir.AluOpType
ACT = mybir.ActivationFunctionType
AX = mybir.AxisListType


def rwkv_moe_layer(nc, x, Wr, Wk, Wv, Wo, decay, ln_w, wg_red, wg, w1, b1, w2, b2, out):
    P = 128
    B, T, D = x.shape
    E, _, HID = w1.shape
    GD = wg_red.shape[0]
    N = B * T
    TILES = N // P
    GT = 4
    G = TILES // GT
    GC = GT * P
    GPB = T // GC
    HC = HID // P
    NT = TILES + E - 1
    REG = N + P
    PAD = E * REG
    C_MEAN, C_RSTD, C_SCORE, C_ID = D, D + 1, D + 2, D + 3
    ROW = D + 4
    LN_EPS, RMS_EPS, GATE_EPS = 1e-5, 1e-6, 1e-4
    NB = 4

    x_v = x.rearrange("b (s p) d -> p (b s) d", p=P)
    out_rows = out.rearrange("b t d -> (b t) d")
    regions = nc.dram_tensor("regions", (PAD + P, ROW), F32).ap()

    ctx = ExitStack()
    with ctx:
        def sb(name, shape, dt=F32):
            return ctx.enter_context(nc.sbuf_tensor(name, shape, dt))

        def pb(name):
            return ctx.enter_context(nc.psum_tensor(name, [P, 512], F32))

        def sem(name):
            return ctx.enter_context(nc.semaphore(name))

        x_all = sb("x_all", [P, TILES, D])
        w1_sb = sb("w1_sb", [P, E * HID])
        w2_sb = sb("w2_sb", [P, E * HID])
        w_nat = sb("w_nat", [P, 4, D])
        wT = sb("wT", [P, 4, D])
        dec_in = sb("dec_in", [P, 1])
        lnw = sb("lnw", [P, 1])
        wgr = sb("wgr", [GD, D])
        wg_sb = sb("wg_sb", [E, GD])
        b1_sp = sb("b1_sp", [P, E * HID // P])
        b2_sp = sb("b2_sp", [E, D])
        b1_part = sb("b1_part", [P, 3, E * HID // P], BF16)
        b2_part = sb("b2_part", [E, 3, D], BF16)
        b1_rows = sb("b1_rows", [3, E * HID], BF16)
        b2_rows = sb("b2_rows", [3, E * HID], BF16)
        ident = sb("ident", [P, P])
        before = sb("before", [P, P], BF16)
        ones_bf = sb("ones_bf", [P, P], BF16)
        mean_w = sb("mean_w", [P, P])
        neg_half = sb("neg_half", [P, TILES])
        half = sb("half", [E, 1])
        ones_col = sb("ones_col", [P, 1])
        t_iota = sb("t_iota", [P, T], I32)
        scale_t = sb("scale_t", [P, T])
        gain = sb("gain", [P, T])
        dec_row = sb("dec_row", [P, T])
        dcol = sb("dcol", [P, 4])
        first_i = sb("first_i", [P, GT, E], I32)
        first_w = sb("first_w", [P, GT, E])
        reg_i = sb("reg_i", [P, GT, E], I32)
        reg_base = sb("reg_base", [P, GT, E])
        fill_i = sb("fill_i", [P, E], I32)
        fill_base = sb("fill_base", [P, E])
        ids = sb("ids", [P, TILES], I32)
        pad_row = sb("pad_row", [P, ROW])
        gsq = sb("gsq", [E, GD])
        gn = sb("gn", [E, 4])
        wgu = sb("wgu", [E, GD])
        wguT = sb("wguT", [GD, E])
        gate_m = sb("gate_m", [P, E])
        gate_c = sb("gate_c", [P, E])
        st1 = sb("st1", [P, TILES, 6])
        ms = sb("ms", [P, 5, TILES])
        rstd1 = sb("rstd1", [P, TILES])
        xn = sb("xn", [P, 2, GT, D])
        xnT = sb("xnT", [P, 2, GC])
        rt = sb("rt", [P, 2, GC])
        vg = sb("vg", [P, GC])
        kv = sb("kv", [P, GC])
        state = sb("state", [P, 2, GC])
        y = sb("y", [P, 2, GC])
        y2 = sb("y2", [P, 2, GC])
        ssm = sb("ssm", [P, 2, GT])
        rrms = sb("rrms", [P, 2, GT])
        rows = sb("rows", [P, TILES, ROW])
        st2 = sb("st2", [P, GT, 6])
        mv2 = sb("mv2", [P, 2, GT, 2])
        ve2 = sb("ve2", [P, 2, GT])
        x1T = sb("x1T", [P, 2, GC])
        lg = sb("lg", [P, GT, E])
        mx = sb("mx", [P, GT])
        dl = sb("dl", [P, 2, GT, E])
        cand = sb("cand", [P, GT, E])
        cmx = sb("cmx", [P, GT])
        oneh = sb("oneh", [P, 2, GT, E], BF16)
        ex = sb("ex", [P, 2, GT, E])
        sx = sb("sx", [P, 2, GT])
        prefix = sb("prefix", [P, TILES + 1, E], BF16)
        pos_f = sb("pos_f", [P, GT, E])
        pos_m = sb("pos_m", [P, GT, E])
        pos = sb("pos", [P, TILES], I32)
        fill_pos = sb("fill_pos", [P, E], I32)
        cnt_i = sb("cnt_i", [1, 2, E], I32)
        tl = sb("tl", [1, E])
        tl_end = sb("tl_end", [1, E])
        ones_row = sb("ones_row", [1, E])
        j_i = sb("j_i", [1, NT, E], I32)
        j_f = sb("j_f", [1, NT, E])
        past = sb("past", [1, NT, E])
        past_t = sb("past_t", [1, NT, E])
        exp_j = sb("exp_j", [1, NT])
        skip_j = sb("skip_j", [1, NT])
        row_a = sb("row_a", [1, NT])
        row_b = sb("row_b", [1, NT])
        tab_row = sb("tab_row", [1, NT], I32)
        tab_off = sb("tab_off", [1, NT], I32)
        xs = [sb(f"xs{k}", [P, ROW]) for k in range(NB)]
        tok = [sb(f"tok{k}", [P, 1], I32) for k in range(NB)]
        ob = [sb(f"ob{k}", [P, D]) for k in range(NB)]
        zn = [sb(f"zn{k}", [P, D]) for k in range(2)]
        znT = [sb(f"znT{k}", [P, P]) for k in range(2)]
        h = [sb(f"h{k}", [P, HID]) for k in range(2)]
        hT = [sb(f"hT{k}", [P, HID]) for k in range(2)]

        banks = [pb(f"bank{n}") for n in range(8)]
        T_ps, R_ps, K_ps, V_ps, O_ps, S_ps, L_ps, C_ps = banks
        up_ps = [R_ps, K_ps]
        hT_ps = [V_ps, O_ps]
        zT_ps = [T_ps, S_ps]
        dn_ps = [L_ps, C_ps]

        x_loaded = [sem(f"x_loaded{g}") for g in range(G)]
        names = """params_loaded ffn_loaded brows_loaded pad_stored consts ident_ready decay_step decay_exp
            wT_ps_ready wT_ready gate_step gate_norm gate_pe gain_ready bias_split
            st1_done ms_step rstd1_ready
            xn_ready xnT_ps_ready xnT_ready rkv_ready r_ready vg_ready kv_ready state_ready y_ready y2_ready
            out_ready ssm_ready rrms_ready x1_ready st2_ready mv2_ready ve2_ready rstd2_ready
            x1T_ps_ready x1T_ready logits_ready lg_ready mx_ready dl_ready cand_ready cmx_ready oneh_ready
            ex_ready sx_ready score_ready prefix_step prefix_ready rank_ready posf_ready posm_ready pos_ready
            id_ready scattered counts_ready fill_ready tab_step tab_ready
            zn_ready zT_ps_ready zT_ready up_ready h_ready hT_ps_ready hT_ready down_ready ob_ready tok_ready
            """.split()
        s = {n: sem(n) for n in names}
        xs_loaded = [sem(f"xs_loaded{k}") for k in range(NB)]
        stored = [sem(f"stored{k}") for k in range(NB)]

        STEPS = G + 4
        SCATTERS = TILES + E
        block = ctx.enter_context(nc.Block())

        @block.sync
        def _(sp):
            for n, w in enumerate((Wr, Wk, Wv, Wo)):
                sp.dma_start(w_nat[:, n, :], w).then_inc(s["params_loaded"], 16)
            sp.dma_start(dec_in[:, :], decay.rearrange("(p a) -> p a", a=1)).then_inc(s["params_loaded"], 16)
            sp.dma_start(lnw[:, :], ln_w.rearrange("(p a) -> p a", a=1)).then_inc(s["params_loaded"], 16)
            sp.dma_start(wgr[:, :], wg_red).then_inc(s["params_loaded"], 16)
            sp.dma_start(wg_sb[:, :], wg).then_inc(s["params_loaded"], 16)
            for g in range(G):
                sp.dma_start(x_all[:, GT * g:GT * g + GT, :], x_v[:, GT * g:GT * g + GT, :]).then_inc(x_loaded[g], 16)
            sp.dma_start(b1_sp[:, :], b1.rearrange("e h -> (e h)").rearrange("(p c) -> p c", p=P)
                         ).then_inc(s["ffn_loaded"], 16)
            sp.dma_start(b2_sp[:, :], b2).then_inc(s["ffn_loaded"], 16)
            sp.wait_ge(s["consts"], 1)
            sp.dma_start(regions[PAD:PAD + P, :], pad_row[:, :]).then_inc(s["pad_stored"], 16)
            sp.wait_ge(s["bias_split"], 10)
            for n in range(3):
                sp.dma_start(b1_rows[n:n + 1, :], b1_part[:, n, :]).then_inc(s["brows_loaded"], 16)
                sp.dma_start(b2_rows[n:n + 1, :].rearrange("a (e h) -> a e h", e=E)[:, :, 0:D],
                             b2_part[:, n, :]).then_inc(s["brows_loaded"], 16)
            for e in range(E):
                sp.dma_start(w1_sb[:, e * HID:(e + 1) * HID], w1[e]).then_inc(s["ffn_loaded"], 16)
                sp.dma_start(w2_sb[:, e * HID:(e + 1) * HID].rearrange("p (c d) -> p c d", c=HC),
                             w2[e].rearrange("(c p) d -> p c d", p=P)).then_inc(s["ffn_loaded"], 16)

            sp.wait_ge(s["tab_ready"], 1)
            sp.wait_ge(s["scattered"], 16 * SCATTERS)
            sp.wait_ge(s["pad_stored"], 16)

            def load(j, k, turn):
                row = sp.value_load(tab_row[0:1, bass.ds(j, 1)], min_val=0, max_val=PAD)
                if turn is not None:
                    sp.wait_ge(s["tok_ready"], j - NB + 1)
                    sp.wait_ge(s["ob_ready"], j - NB + 1)
                sp.dma_start(xs[k][:, :], regions[bass.ds(row, P), :]).then_inc(xs_loaded[k], 16)

            for k in range(NB):
                load(k, k, None)
            with sp.Fori(1, NT // NB) as i:
                for k in range(NB):
                    load(i * NB + k, k, i)
            for j in range(NT // NB * NB, NT):
                load(j, j % NB, j // NB)

        @block.gpsimd
        def _(pool):
            gp = nc.gpsimd
            gp.memset(pad_row[:, :], 0.0).then_inc(s["id_ready"], 1)
            pool.wait_ge(s["id_ready"], 1)
            gp.memset(pad_row[:, C_ID:C_ID + 1].bitcast(I32), 1 << 20).then_inc(s["consts"], 1)
            gp.memset(ident[:, :], 0.0).then_inc(s["ident_ready"], 1)
            pool.wait_ge(s["ident_ready"], 1)
            gp.affine_select(out=ident[:, :], in_=ident[:, :], compare_op=ALU.not_equal, fill=1.0, base=0,
                             pattern=[[-1, P]], channel_multiplier=1).then_inc(s["ident_ready"], 1)
            gp.iota(t_iota[:, :], pattern=[[1, T]], base=0, channel_multiplier=0).then_inc(s["decay_step"], 1)
            gp.memset(neg_half[:, :], -0.5)
            gp.memset(half[:, :], 0.5)
            gp.memset(ones_col[:, :], 1.0)
            gp.memset(ones_bf[:, :], 1.0).then_inc(s["consts"], 1)
            pool.wait_ge(s["consts"], 2)
            gp.affine_select(out=before[:, :], in_=ones_bf[:, :], compare_op=ALU.is_gt, fill=0.0, base=0,
                             pattern=[[1, P]], channel_multiplier=-1)
            gp.memset(mean_w[:, :], 1.0 / D)
            gp.memset(prefix[:, 0, :], 0.0)
            gp.iota(first_i[:, :, :], pattern=[[0, GT], [-1, E]], base=E, channel_multiplier=0)
            gp.iota(reg_i[:, :, :], pattern=[[0, GT], [REG, E]], base=0, channel_multiplier=0)
            gp.iota(fill_i[:, :], pattern=[[REG, E]], base=0, channel_multiplier=1)
            gp.iota(j_i[:, :, :], pattern=[[1, NT], [0, E]], base=0, channel_multiplier=0)
            gp.memset(ones_row[:, :], 1.0)
            gp.iota(ids[:, :], pattern=[[P, TILES]], base=0, channel_multiplier=1).then_inc(s["consts"], 1)
            pool.wait_ge(s["consts"], 3)
            gp.tensor_copy(rows[:, :, C_ID].bitcast(I32), ids[:, :])
            gp.tensor_copy(first_w[:, :, :], first_i[:, :, :])
            gp.tensor_copy(reg_base[:, :, :], reg_i[:, :, :])
            gp.tensor_copy(fill_base[:, :], fill_i[:, :])
            gp.tensor_copy(j_f[:, :, :], j_i[:, :, :]).then_inc(s["consts"], 1)
            pool.wait_ge(s["gate_step"], 2)
            gp.tensor_tensor(gn[:, 1:2], gn[:, 0:1], half[:, :], op=ALU.pow).then_inc(s["gate_norm"], 1)
            pool.wait_ge(s["ms_step"], 4)
            gp.tensor_tensor(rstd1[:, :], ms[:, 4, :], neg_half[:, :], op=ALU.pow).then_inc(s["rstd1_ready"], 1)

            def rms(g):
                pool.wait_ge(s["ssm_ready"], g + 1)
                gp.tensor_tensor(rrms[:, g % 2, :], ssm[:, g % 2, :], neg_half[:, 0:GT], op=ALU.pow
                                 ).then_inc(s["rrms_ready"], 1)

            def squares(g):
                pool.wait_ge(s["y_ready"], g + 1)
                if g >= 2:
                    pool.wait_ge(s["out_ready"], g - 1)
                gp.tensor_tensor(y2[:, g % 2, :], y[:, g % 2, :], y[:, g % 2, :], op=ALU.mult
                                 ).then_inc(s["y2_ready"], 1)

            def ln2(g):
                t0 = GT * g
                pool.wait_ge(s["mv2_ready"], g + 1)
                gp.tensor_copy(rows[:, t0:t0 + GT, C_MEAN], mv2[:, g % 2, :, 0])
                gp.tensor_scalar(ve2[:, g % 2, :], mv2[:, g % 2, :, 1], LN_EPS, None, ALU.add
                                 ).then_inc(s["ve2_ready"], 1)
                pool.wait_ge(s["ve2_ready"], g + 1)
                gp.tensor_tensor(rows[:, t0:t0 + GT, C_RSTD], ve2[:, g % 2, :], neg_half[:, 0:GT], op=ALU.pow
                                 ).then_inc(s["rstd2_ready"], 1)

            def prefixes(g):
                pool.wait_ge(s["oneh_ready"], g + 1)
                for n in range(GT):
                    t = GT * g + n
                    gp.tensor_tensor(prefix[:, t + 1, :], prefix[:, t, :], oneh[:, g % 2, n, :], op=ALU.add
                                     ).then_inc(s["prefix_step"], 1)
                    pool.wait_ge(s["prefix_step"], t + 1)
                gp.engine_nop().then_inc(s["prefix_ready"], 1)

            def scatter(g):
                pool.wait_ge(s["pos_ready"], g + 1)
                pool.wait_ge(s["score_ready"], g + 1)
                for n in range(GT):
                    t = GT * g + n
                    gp.indirect_dma_start(out=regions, out_offset=bass.IndirectOffsetOnAxis(ap=pos[:, t:t + 1], axis=0),
                                          in_=rows[:, t, :], in_offset=None,
                                          bounds_check=PAD - 1, oob_is_err=False).then_inc(s["scattered"], 16)

            for st in range(STEPS):
                if 0 <= st - 2 < G:
                    rms(st - 2)
                if 0 <= st - 1 < G:
                    squares(st - 1)
                if 0 <= st - 3 < G:
                    prefixes(st - 3)
                if 0 <= st - 4 < G:
                    scatter(st - 4)
                if 0 <= st - 2 < G:
                    ln2(st - 2)
            pool.wait_ge(s["fill_ready"], 1)
            for e in range(E):
                gp.indirect_dma_start(out=regions, out_offset=bass.IndirectOffsetOnAxis(ap=fill_pos[:, e:e + 1], axis=0),
                                      in_=pad_row[:, :], in_offset=None,
                                      bounds_check=PAD - 1, oob_is_err=False).then_inc(s["scattered"], 16)

            def token_numbers(j, k, turn):
                pool.wait_ge(xs_loaded[k], turn * 16 + 16)
                if turn > 0:
                    pool.wait_ge(stored[k], turn * 16)
                gp.tensor_copy(tok[k][:, :], xs[k][:, C_ID:C_ID + 1].bitcast(I32)).then_inc(s["tok_ready"], 1)

            def store(j, k, turn):
                pool.wait_ge(s["ob_ready"], j + 1)
                pool.wait_ge(s["tok_ready"], j + 1)
                gp.indirect_dma_start(out=out_rows, out_offset=bass.IndirectOffsetOnAxis(ap=tok[k][:, 0:1], axis=0),
                                      in_=ob[k][:, :], in_offset=None,
                                      bounds_check=N - 1, oob_is_err=False).then_inc(stored[k], 16)

            token_numbers(0, 0, 0)
            for k in range(NB - 1):
                token_numbers(k + 1, k + 1, 0)
                store(k, k, 0)
            for j in range(NB, NT):
                token_numbers(j, j % NB, j // NB)
                store(j - 1, (j - 1) % NB, None)
            store(NT - 1, (NT - 1) % NB, None)
            for k in range(NB):
                pool.wait_ge(stored[k], 16 * len(range(k, NT, NB)))

        @block.scalar
        def _(act):
            ac = nc.scalar
            act.wait_ge(s["params_loaded"], 128)
            ac.activation(dcol[:, 0:1], dec_in[:, :], ACT.Exp, scale=-1.0).then_inc(s["decay_exp"], 1)
            act.wait_ge(s["decay_step"], 4)
            ac.activation(dcol[:, 3:4], dcol[:, 2:3], ACT.Ln).then_inc(s["decay_exp"], 1)
            act.wait_ge(s["decay_exp"], 2)
            ac.activation(scale_t[:, :], t_iota[:, :], ACT.Exp, scale=dcol[:, 3:4]).then_inc(s["decay_exp"], 1)

            def evac_xn(g):
                act.wait_ge(s["xnT_ps_ready"], g + 1)
                if g >= 2:
                    act.wait_ge(s["rkv_ready"], 2 * (g - 1))
                ac.copy(xnT[:, g % 2, :], T_ps[:, :]).then_inc(s["xnT_ready"], 1)

            def tanh_r(g):
                act.wait_ge(s["rkv_ready"], 2 * g + 2)
                if g >= 2:
                    act.wait_ge(s["y_ready"], g - 1)
                ac.activation(rt[:, g % 2, :], R_ps[:, :], ACT.Tanh, scale=0.5).then_inc(s["r_ready"], 1)

            def evac_x1(g):
                act.wait_ge(s["x1T_ps_ready"], g + 1)
                if g >= 2:
                    act.wait_ge(s["logits_ready"], g - 1)
                ac.copy(x1T[:, g % 2, :], T_ps[:, :]).then_inc(s["x1T_ready"], 1)

            def exps(g):
                act.wait_ge(s["dl_ready"], g + 1)
                if g >= 2:
                    act.wait_ge(s["sx_ready"], g - 1)
                ac.activation(ex[:, g % 2, :, :], dl[:, g % 2, :, :], ACT.Exp).then_inc(s["ex_ready"], 1)

            for st in range(STEPS):
                if 0 <= st < G:
                    evac_xn(st)
                if 0 <= st - 3 < G:
                    exps(st - 3)
                if 0 <= st < G:
                    tanh_r(st)
                if 0 <= st - 2 < G:
                    evac_x1(st - 2)

            def evac_z(j, k, first):
                act.wait_ge(s["zT_ps_ready"], j + 1)
                if not first:
                    act.wait_ge(s["up_ready"], j - 1)
                ac.copy(znT[k % 2][:, :], zT_ps[k % 2][:, 0:P]).then_inc(s["zT_ready"], 1)

            def gelu(j, k, first):
                act.wait_ge(s["up_ready"], j + 1)
                if not first:
                    act.wait_ge(s["hT_ps_ready"], j - 1)
                ac.activation(h[k % 2][:, :], up_ps[k % 2][:, :], ACT.Gelu).then_inc(s["h_ready"], 1)

            evac_z(0, 0, True)
            gelu(0, 0, True)
            evac_z(1, 1, True)
            gelu(1, 1, True)
            evac_z(2, 0, False)
            loops = (NT - 2) // NB
            with act.Fori(0, loops) as i:
                for k in range(NB):
                    gelu(i * NB + 2 + k, k, False)
                    evac_z(i * NB + 3 + k, 1 + k, False)
            for j in range(loops * NB + 2, NT):
                gelu(j, j, False)
                if j + 1 < NT:
                    evac_z(j + 1, j + 1, False)

        @block.vector
        def _(dve):
            ve = nc.vector
            dve.wait_ge(s["decay_exp"], 1)
            ve.tensor_scalar(dcol[:, 1:2], dcol[:, 0:1], 1.0, None, ALU.add).then_inc(s["decay_step"], 1)
            dve.wait_ge(s["decay_step"], 2)
            ve.reciprocal(dcol[:, 0:1], dcol[:, 1:2]).then_inc(s["decay_step"], 1)
            dve.wait_ge(s["decay_step"], 3)
            ve.tensor_scalar(dcol[:, 2:3], dcol[:, 0:1], 1e-7, None, ALU.max).then_inc(s["decay_step"], 1)
            dve.wait_ge(s["params_loaded"], 128)
            ve.tensor_tensor(gsq[:, :], wg_sb[:, :], wg_sb[:, :], ALU.mult).then_inc(s["gate_step"], 1)
            dve.wait_ge(s["gate_step"], 1)
            ve.tensor_reduce(gn[:, 0:1], gsq[:, :], AX.X, ALU.add).then_inc(s["gate_step"], 1)
            dve.wait_ge(s["wT_ps_ready"], 1)
            ve.tensor_copy(wT[:, 0:3, :], T_ps[:, 0:3 * D].rearrange("p (a b) -> p a b", a=3))
            ve.tensor_scalar(wT[:, 3, :], T_ps[:, 3 * D:4 * D], lnw[:, 0:1], None, ALU.mult).then_inc(s["wT_ready"], 1)
            for g in range(G):
                dve.wait_ge(x_loaded[g], 16)
                for n in range(GT * g, GT * g + GT):
                    last = ve.bn_stats(st1[:, n, :], x_all[:, n, :])
            last.then_inc(s["st1_done"], 1)
            dve.wait_ge(s["st1_done"], 1)
            ve.tensor_tensor(ms[:, 0, :], st1[:, :, 1], st1[:, :, 4], ALU.add)
            ve.tensor_tensor(ms[:, 1, :], st1[:, :, 1], st1[:, :, 4], ALU.subtract)
            ve.tensor_tensor(ms[:, 2, :], st1[:, :, 2], st1[:, :, 5], ALU.add).then_inc(s["ms_step"], 1)
            dve.wait_ge(s["ms_step"], 1)
            ve.tensor_tensor(ms[:, 3, :], ms[:, 1, :], ms[:, 1, :], ALU.mult)
            ve.tensor_scalar(ms[:, 4, :], ms[:, 2, :], 1.0 / D, LN_EPS, ALU.mult, ALU.add).then_inc(s["ms_step"], 1)
            dve.wait_ge(s["ms_step"], 2)
            ve.tensor_scalar(ms[:, 1, :], ms[:, 3, :], 0.25, None, ALU.mult)
            ve.tensor_scalar(ms[:, 2, :], ms[:, 0, :], 0.5, None, ALU.mult).then_inc(s["ms_step"], 1)
            dve.wait_ge(s["ms_step"], 3)
            ve.tensor_tensor(ms[:, 4, :], ms[:, 4, :], ms[:, 1, :], ALU.add).then_inc(s["ms_step"], 1)
            dve.wait_ge(s["decay_exp"], 3)
            ve.tensor_scalar(gain[:, :], scale_t[:, :], 0.5e10, 0.5, ALU.mult, ALU.min)
            ve.tensor_scalar(dec_row[:, :], scale_t[:, :], 0.0, dcol[:, 2:3], ALU.mult, ALU.add
                             ).then_inc(s["gain_ready"], 1)
            dve.wait_ge(s["gain_ready"], 1)
            ve.memset(dec_row[:, 0:1], 0.0)
            ve.memset(state[:, 1, GC - 1:GC], 0.0).then_inc(s["gain_ready"], 1)
            dve.wait_ge(s["gate_norm"], 1)
            ve.tensor_scalar(gn[:, 2:3], gn[:, 1:2], GATE_EPS, None, ALU.max).then_inc(s["gate_step"], 1)
            dve.wait_ge(s["gate_step"], 3)
            ve.reciprocal(gn[:, 3:4], gn[:, 2:3]).then_inc(s["gate_step"], 1)
            dve.wait_ge(s["gate_step"], 4)
            ve.tensor_scalar(wgu[:, :], wg_sb[:, :], gn[:, 3:4], None, ALU.mult).then_inc(s["gate_step"], 1)
            dve.wait_ge(s["gate_pe"], 1)
            ve.tensor_copy(wguT[:, :], S_ps[0:GD, 0:E]).then_inc(s["gate_step"], 1)
            dve.wait_ge(s["gate_pe"], 2)
            ve.tensor_copy(gate_m[:, :], L_ps[:, 0:E]).then_inc(s["gate_step"], 1)
            dve.wait_ge(s["gate_pe"], 3)
            dve.wait_ge(s["gate_step"], 7)
            ve.tensor_tensor(gate_c[:, :], gate_m[:, :], C_ps[:, 0:E], ALU.subtract).then_inc(s["gate_step"], 1)
            dve.wait_ge(s["gain_ready"], 2)
            dve.wait_ge(s["consts"], 4)
            dve.wait_ge(s["rstd1_ready"], 1)

            def mean_square(g):
                dve.wait_ge(s["out_ready"], g + 1)
                ve.tensor_scalar(ssm[:, g % 2, :], S_ps[:, 0:GT], 1.0 / D, RMS_EPS, ALU.mult, ALU.add
                                 ).then_inc(s["ssm_ready"], 1)

            def normalise(g):
                if g >= 2:
                    dve.wait_ge(s["xnT_ps_ready"], g - 1)
                for n in range(GT):
                    t = GT * g + n
                    last = ve.tensor_scalar(xn[:, g % 2, n, :], x_all[:, t, :], ms[:, 2, t:t + 1], rstd1[:, t:t + 1],
                                            ALU.subtract, ALU.mult)
                last.then_inc(s["xn_ready"], 1)

            def recur(g):
                c = g % GPB * GC
                dve.wait_ge(s["rkv_ready"], 2 * g + 1)
                ve.tensor_tensor(vg[:, :], V_ps[:, :], gain[:, c:c + GC], ALU.mult).then_inc(s["vg_ready"], 1)
                dve.wait_ge(s["vg_ready"], g + 1)
                ve.tensor_tensor(kv[:, :], K_ps[:, :], vg[:, :], ALU.mult).then_inc(s["kv_ready"], 1)
                dve.wait_ge(s["kv_ready"], g + 1)
                ve.tensor_tensor_scan(state[:, g % 2, :], dec_row[:, c:c + GC], kv[:, :],
                                      state[:, (g + 1) % 2, GC - 1:GC], ALU.mult, ALU.add
                                      ).then_inc(s["state_ready"], 1)
                dve.wait_ge(s["state_ready"], g + 1)
                dve.wait_ge(s["r_ready"], g + 1)
                if g >= 2:
                    dve.wait_ge(s["out_ready"], g - 1)
                ve.scalar_tensor_tensor(y[:, g % 2, :], rt[:, g % 2, :], 1.0, state[:, g % 2, :],
                                        ALU.add, ALU.mult).then_inc(s["y_ready"], 1)

            def residual(g):
                dve.wait_ge(s["rrms_ready"], g + 1)
                for n in range(GT):
                    t = GT * g + n
                    last = ve.scalar_tensor_tensor(rows[:, t, 0:D], O_ps[:, n * D:(n + 1) * D], rrms[:, g % 2, n:n + 1],
                                                   x_all[:, t, :], ALU.mult, ALU.add)
                last.then_inc(s["x1_ready"], 1)
                dve.wait_ge(s["x1_ready"], g + 1)
                for n in range(GT):
                    last = ve.bn_stats(st2[:, n, :], rows[:, GT * g + n, 0:D])
                last.then_inc(s["st2_ready"], 1)
                dve.wait_ge(s["st2_ready"], g + 1)
                if g >= 2:
                    dve.wait_ge(s["rstd2_ready"], g - 1)
                for n in range(GT):
                    last = ve.bn_aggr(mv2[:, g % 2, n, :], st2[:, n, :])
                last.then_inc(s["mv2_ready"], 1)

            def choose(g):
                t0 = GT * g
                dve.wait_ge(s["logits_ready"], g + 1)
                dve.wait_ge(s["rstd2_ready"], g + 1)
                ve.tensor_tensor(lg[:, :, :], L_ps[:, 0:GT * E].rearrange("p (a b) -> p a b", a=GT),
                                 rows[:, t0:t0 + GT, C_RSTD:C_RSTD + 1].broadcast_to([P, GT, E]),
                                 ALU.mult).then_inc(s["lg_ready"], 1)
                dve.wait_ge(s["lg_ready"], g + 1)
                ve.tensor_reduce(mx[:, :], lg[:, :, :], AX.X, ALU.max).then_inc(s["mx_ready"], 1)
                dve.wait_ge(s["mx_ready"], g + 1)
                if g >= 2:
                    dve.wait_ge(s["ex_ready"], g - 1)
                ve.tensor_tensor(dl[:, g % 2, :, :], lg[:, :, :], mx[:, :].unsqueeze(2).broadcast_to([P, GT, E]),
                                 ALU.subtract).then_inc(s["dl_ready"], 1)
                dve.wait_ge(s["dl_ready"], g + 1)
                ve.scalar_tensor_tensor(cand[:, :, :], dl[:, g % 2, :, :], 0.0, first_w[:, :, :],
                                        ALU.is_equal, ALU.mult).then_inc(s["cand_ready"], 1)
                dve.wait_ge(s["cand_ready"], g + 1)
                ve.tensor_reduce(cmx[:, :], cand[:, :, :], AX.X, ALU.max).then_inc(s["cmx_ready"], 1)
                dve.wait_ge(s["cmx_ready"], g + 1)
                ve.tensor_tensor(oneh[:, g % 2, :, :], cand[:, :, :], cmx[:, :].unsqueeze(2).broadcast_to([P, GT, E]),
                                 ALU.is_equal).then_inc(s["oneh_ready"], 1)
                dve.wait_ge(s["ex_ready"], g + 1)
                ve.tensor_reduce(sx[:, g % 2, :], ex[:, g % 2, :, :], AX.X, ALU.add).then_inc(s["sx_ready"], 1)
                dve.wait_ge(s["sx_ready"], g + 1)
                ve.reciprocal(rows[:, t0:t0 + GT, C_SCORE], sx[:, g % 2, :]).then_inc(s["score_ready"], 1)

            def place(g):
                dve.wait_ge(s["rank_ready"], g + 1)
                ve.tensor_tensor(pos_f[:, :, :], C_ps[:, 0:GT * E].rearrange("p (a b) -> p a b", a=GT),
                                 reg_base[:, :, :], ALU.add).then_inc(s["posf_ready"], 1)
                dve.wait_ge(s["posf_ready"], g + 1)
                ve.tensor_tensor(pos_m[:, :, :], pos_f[:, :, :], oneh[:, g % 2, :, :], ALU.mult
                                 ).then_inc(s["posm_ready"], 1)
                dve.wait_ge(s["posm_ready"], g + 1)
                with nc.allow_low_precision(reason="whole numbers"):
                    ve.tensor_reduce(pos[:, GT * g:GT * g + GT], pos_m[:, :, :], AX.X, ALU.add
                                     ).then_inc(s["pos_ready"], 1)

            for st in range(STEPS):
                if 0 <= st - 2 < G:
                    mean_square(st - 2)
                if 0 <= st < G:
                    normalise(st)
                if 0 <= st - 4 < G:
                    place(st - 4)
                if 0 <= st - 1 < G:
                    recur(st - 1)
                if 0 <= st - 2 < G:
                    residual(st - 2)
                if 0 <= st - 3 < G:
                    choose(st - 3)
                if st == 2:
                    dve.wait_ge(s["ffn_loaded"], 32)
                    n = 0
                    for full, part in ((b1_sp, b1_part), (b2_sp, b2_part)):
                        for m in range(3):
                            ve.tensor_copy(part[:, m, :], full[:, :]).then_inc(s["bias_split"], 1)
                            n += 1
                            dve.wait_ge(s["bias_split"], n)
                            if m < 2:
                                ve.tensor_tensor(full[:, :], full[:, :], part[:, m, :], ALU.subtract
                                                 ).then_inc(s["bias_split"], 1)
                                n += 1
                                dve.wait_ge(s["bias_split"], n)

            dve.wait_ge(s["counts_ready"], 1)
            with nc.allow_low_precision(reason="whole numbers"):
                ve.tensor_tensor(fill_pos[:, :], L_ps[:, 0:E], fill_base[:, :], ALU.add).then_inc(s["fill_ready"], 1)
                ve.tensor_scalar(cnt_i[0:1, 0, :], L_ps[0:1, 0:E], float(P - 1), None, ALU.add
                                 ).then_inc(s["tab_step"], 1)
                dve.wait_ge(s["tab_step"], 1)
                ve.tensor_scalar(cnt_i[0:1, 1, :], cnt_i[0:1, 0, :], 7, None, ALU.arith_shift_right
                                 ).then_inc(s["tab_step"], 1)
            dve.wait_ge(s["tab_step"], 2)
            ve.tensor_copy(tl[:, :], cnt_i[0:1, 1, :]).then_inc(s["tab_step"], 1)
            dve.wait_ge(s["tab_step"], 3)
            ve.tensor_tensor_scan(tl_end[:, :], ones_row[:, :], tl[:, :], 0.0, ALU.mult, ALU.add
                                  ).then_inc(s["tab_step"], 1)
            dve.wait_ge(s["tab_step"], 4)
            ve.tensor_tensor(past[:, :, :], j_f[:, :, :], tl_end[:, :].unsqueeze(1).broadcast_to([1, NT, E]),
                             ALU.is_ge).then_inc(s["tab_step"], 1)
            dve.wait_ge(s["tab_step"], 5)
            ve.tensor_tensor(past_t[:, :, :], past[:, :, :], tl[:, :].unsqueeze(1).broadcast_to([1, NT, E]),
                             ALU.mult)
            ve.tensor_reduce(exp_j[:, :], past[:, :, :], AX.X, ALU.add).then_inc(s["tab_step"], 1)
            dve.wait_ge(s["tab_step"], 6)
            ve.tensor_reduce(skip_j[:, :], past_t[:, :, :], AX.X, ALU.add).then_inc(s["tab_step"], 1)
            dve.wait_ge(s["tab_step"], 7)
            ve.tensor_tensor(row_a[:, :], j_f[:, :, 0], skip_j[:, :], ALU.subtract)
            ve.tensor_scalar(row_b[:, :], exp_j[:, :], float(REG), None, ALU.mult).then_inc(s["tab_step"], 1)
            dve.wait_ge(s["tab_step"], 8)
            ve.scalar_tensor_tensor(row_b[:, :], row_a[:, :], float(P), row_b[:, :], ALU.mult, ALU.add
                                    ).then_inc(s["tab_step"], 1)
            dve.wait_ge(s["tab_step"], 9)
            with nc.allow_low_precision(reason="whole numbers"):
                ve.tensor_scalar(tab_off[:, :], exp_j[:, :], float(E - 1), float(HID), ALU.min, ALU.mult)
                ve.tensor_scalar(tab_row[:, :], row_b[:, :], float(PAD), None, ALU.min).then_inc(s["tab_ready"], 1)

            def norm_z(j, k, turn, first):
                dve.wait_ge(xs_loaded[k], turn * 16 + 16)
                if not first:
                    dve.wait_ge(s["zT_ps_ready"], j - 1)
                ve.tensor_scalar(zn[k % 2][:, :], xs[k][:, 0:D], xs[k][:, C_MEAN:C_MEAN + 1],
                                 xs[k][:, C_RSTD:C_RSTD + 1], ALU.subtract, ALU.mult).then_inc(s["zn_ready"], 1)

            def evac_h(j, k, first):
                dve.wait_ge(s["hT_ps_ready"], j + 1)
                if not first:
                    dve.wait_ge(s["down_ready"], j - 1)
                ve.tensor_copy(hT[k % 2][:, :], hT_ps[k % 2][:, :]).then_inc(s["hT_ready"], 1)

            def finish(j, k, turn, first):
                dve.wait_ge(s["down_ready"], j + 1)
                if not first:
                    dve.wait_ge(stored[k], turn * 16)
                ve.scalar_tensor_tensor(ob[k][:, :], dn_ps[k % 2][:, 0:D], xs[k][:, C_SCORE:C_SCORE + 1],
                                        xs[k][:, 0:D], ALU.mult, ALU.add).then_inc(s["ob_ready"], 1)

            norm_z(0, 0, 0, True)
            norm_z(1, 1, 0, True)
            for j in range(NB + 1):
                evac_h(j, j, j < 2)
                norm_z(j + 2, (j + 2) % NB, (j + 2) // NB, False)
                if j >= 1:
                    finish(j - 1, j - 1, 0, True)
            loops = (NT - 3) // NB
            with dve.Fori(1, loops) as i:
                for k in range(NB):
                    j = i * NB + 1 + k
                    evac_h(j, 1 + k, False)
                    norm_z(j + 2, (3 + k) % NB, i + (3 + k) // NB, False)
                    finish(j - 1, k, i, False)
            for j in range(loops * NB + 1, NT):
                evac_h(j, j, False)
                if j + 2 < NT:
                    norm_z(j + 2, (j + 2) % NB, (j + 2) // NB, False)
                finish(j - 1, (j - 1) % NB, (j - 1) // NB, False)
            finish(NT - 1, (NT - 1) % NB, (NT - 1) // NB, False)

        @block.tensor
        def _(pe):
            te = nc.tensor
            pe.wait_ge(s["params_loaded"], 128)
            pe.wait_ge(s["ident_ready"], 2)
            for n in range(4):
                last = te.transpose(T_ps[:, n * D:(n + 1) * D], w_nat[:, n, :], ident[:, :])
            last.then_inc(s["wT_ps_ready"], 1)
            pe.wait_ge(s["gate_step"], 5)
            te.transpose(S_ps[0:GD, 0:E], wgu[:, :], ident[0:E, 0:E]).then_inc(s["gate_pe"], 1)
            pe.wait_ge(s["gate_step"], 6)
            te.matmul(L_ps[:, 0:E], wgr[:, :], wguT[:, :], start=True, stop=True).then_inc(s["gate_pe"], 1)
            pe.wait_ge(s["gate_step"], 7)
            pe.wait_ge(s["consts"], 3)
            te.matmul(C_ps[:, 0:E], mean_w[:, :], gate_m[:, :], start=True, stop=True).then_inc(s["gate_pe"], 1)
            pe.wait_ge(s["wT_ready"], 1)

            def project_out(g):
                pe.wait_ge(s["y_ready"], g + 1)
                pe.wait_ge(s["y2_ready"], g + 1)
                if g >= 1:
                    pe.wait_ge(s["x1_ready"], g)
                for n in range(GT):
                    te.matmul(O_ps[:, n * D:(n + 1) * D], y[:, g % 2, n * P:(n + 1) * P], wT[:, 3, :],
                              start=True, stop=True)
                for n in range(GT):
                    last = te.matmul(S_ps[:, n:n + 1], y2[:, g % 2, n * P:(n + 1) * P], ones_col[:, :],
                                     start=True, stop=True)
                last.then_inc(s["out_ready"], 1)



            def turn_xn(g):
                pe.wait_ge(s["xn_ready"], g + 1)
                if g >= 3:
                    pe.wait_ge(s["x1T_ready"], g - 2)
                elif g >= 1:
                    pe.wait_ge(s["xnT_ready"], g)
                for n in range(GT):
                    last = te.transpose(T_ps[:, n * P:(n + 1) * P], xn[:, g % 2, n, :], ident[:, :])
                last.then_inc(s["xnT_ps_ready"], 1)

            def project_in(g):
                pe.wait_ge(s["xnT_ready"], g + 1)
                if g >= 1:
                    pe.wait_ge(s["kv_ready"], g)
                te.matmul(V_ps[:, :], wT[:, 2, :], xnT[:, g % 2, :], start=True, stop=True)
                te.matmul(K_ps[:, :], wT[:, 1, :], xnT[:, g % 2, :], start=True, stop=True
                          ).then_inc(s["rkv_ready"], 1)
                if g >= 1:
                    pe.wait_ge(s["r_ready"], g)
                te.matmul(R_ps[:, :], wT[:, 0, :], xnT[:, g % 2, :], start=True, stop=True
                          ).then_inc(s["rkv_ready"], 1)

            def turn_x1(g):
                pe.wait_ge(s["x1_ready"], g + 1)
                pe.wait_ge(s["xnT_ready"], min(g + 3, G))
                for n in range(GT):
                    last = te.transpose(T_ps[:, n * P:(n + 1) * P], rows[:, GT * g + n, 0:D], ident[:, :])
                last.then_inc(s["x1T_ps_ready"], 1)

            def logits(g):
                pe.wait_ge(s["x1T_ready"], g + 1)
                pe.wait_ge(s["gate_step"], 8)
                if g >= 1:
                    pe.wait_ge(s["lg_ready"], g)
                for n in range(GT):
                    last = te.matmul(L_ps[:, n * E:(n + 1) * E], x1T[:, g % 2, n * P:(n + 1) * P], gate_c[:, :],
                                     start=True, stop=True)
                last.then_inc(s["logits_ready"], 1)

            def ranks(g):
                pe.wait_ge(s["oneh_ready"], g + 1)
                pe.wait_ge(s["prefix_ready"], g + 1)
                if g >= 1:
                    pe.wait_ge(s["posf_ready"], g)
                te.matmul(C_ps[:, 0:GT * E], before[:, :], oneh[:, g % 2, :, :].rearrange("p a b -> p (a b)"),
                          start=True, stop=False)
                te.matmul(C_ps[:, 0:GT * E], ones_bf[:, :],
                          prefix[:, GT * g:GT * g + GT, :].rearrange("p a b -> p (a b)"),
                          start=False, stop=True).then_inc(s["rank_ready"], 1)

            for st in range(STEPS):
                if 0 <= st - 2 < G:
                    project_out(st - 2)
                if 0 <= st < G:
                    turn_xn(st)
                    project_in(st)
                if 0 <= st - 2 < G:
                    turn_x1(st - 2)
                    logits(st - 2)
                if 0 <= st - 3 < G:
                    ranks(st - 3)
            pe.wait_ge(s["lg_ready"], G)
            te.matmul(L_ps[:, 0:E], ones_bf[:, :], prefix[:, TILES, :], start=True, stop=True
                      ).then_inc(s["counts_ready"], 1)

            pe.wait_ge(s["tab_ready"], 1)
            pe.wait_ge(s["ffn_loaded"], 16 * (2 + 2 * E))
            pe.wait_ge(s["brows_loaded"], 16 * 6)

            def expert_of(j):
                return pe.value_load(tab_off[0:1, bass.ds(j, 1)], min_val=0, max_val=(E - 1) * HID)

            def turn_z(j, k):
                pe.wait_ge(s["zn_ready"], j + 1)
                te.transpose(zT_ps[k % 2][:, 0:P], zn[k % 2][:, :], ident[:, :]).then_inc(s["zT_ps_ready"], 1)

            def up(j, k, first):
                off = expert_of(j)
                pe.wait_ge(s["zT_ready"], j + 1)
                te.matmul(up_ps[k % 2][:, :], ones_bf[0:3, :], b1_rows[:, bass.ds(off, HID)], start=True, stop=False)
                te.matmul(up_ps[k % 2][:, :], znT[k % 2][:, :], w1_sb[:, bass.ds(off, HID)], start=False, stop=True
                          ).then_inc(s["up_ready"], 1)

            def turn_h(j, k):
                pe.wait_ge(s["h_ready"], j + 1)
                for c in range(HC):
                    last = te.transpose(hT_ps[k % 2][:, c * P:(c + 1) * P], h[k % 2][:, c * P:(c + 1) * P], ident[:, :])
                last.then_inc(s["hT_ps_ready"], 1)

            def down(j, k, first):
                off = expert_of(j)
                pe.wait_ge(s["hT_ready"], j + 1)
                if not first:
                    pe.wait_ge(s["ob_ready"], j - 1)
                te.matmul(dn_ps[k % 2][:, 0:D], ones_bf[0:3, :], b2_rows[:, bass.ds(off, D)], start=True, stop=False)
                for c in range(HC):
                    last = te.matmul(dn_ps[k % 2][:, 0:D], hT[k % 2][:, c * P:(c + 1) * P],
                                     w2_sb[:, bass.ds(off + c * D, D)], start=False, stop=(c == HC - 1))
                last.then_inc(s["down_ready"], 1)

            turn_z(0, 0)
            up(0, 0, True)
            turn_z(1, 1)
            for j in range(1, 3):
                turn_h(j - 1, j - 1)
                up(j, j, True)
                down(j - 1, j - 1, True)
                turn_z(j + 1, j + 1)
            loops = (NT - 4) // NB
            with pe.Fori(0, loops) as i:
                for k in range(3, 3 + NB):
                    j = i * NB + k
                    turn_h(j - 1, k - 1)
                    up(j, k, False)
                    down(j - 1, k - 1, False)
                    turn_z(j + 1, k + 1)
            for j in range(loops * NB + 3, NT + 1):
                turn_h(j - 1, j - 1)
                if j < NT:
                    up(j, j, False)
                down(j - 1, j - 1, False)
                if j + 1 < NT:
                    turn_z(j + 1, j + 1)


_INS = ['L0_attn_x', 'L0_attn_Wr', 'L0_attn_Wk', 'L0_attn_Wv', 'L0_attn_Wo', 'L0_attn_decay', 'L0_attn_ln_w',
        'L0_ffn_wg_red', 'L0_ffn_wg', 'L0_ffn_w1', 'L0_ffn_b1', 'L0_ffn_w2', 'L0_ffn_b2']


def kernel(**inputs):
    import numpy as _np
    import concourse.bacc as _bacc
    from concourse import mybir as _mybir
    from concourse.bass_utils import run_bass_kernel_spmd as _run

    nc = _bacc.Bacc("TRN2", target_bir_lowering=False, num_devices=1)
    arrays, args = {}, []
    for name in _INS:
        a = _np.ascontiguousarray(inputs[name])
        arrays[f"in_{name}_dram"] = a
        args.append(nc.dram_tensor(f"in_{name}_dram", a.shape, _mybir.dt.from_np(a.dtype), kind="ExternalInput").ap())
    shape = inputs['L0_attn_x'].shape
    args.append(nc.dram_tensor("out_0_dram", shape, _mybir.dt.float32, kind="ExternalOutput").ap())
    rwkv_moe_layer(nc, *args)
    r = _run(nc, [arrays], core_ids=[0])
    return r.results[0]["out_0_dram"]
```

```python
import concourse.bass as bass
from concourse import mybir
from contextlib import ExitStack

F32 = mybir.dt.float32
BF16 = mybir.dt.bfloat16
I32 = mybir.dt.int32
ALU = mybir.AluOpType
ACT = mybir.ActivationFunctionType
AX = mybir.AxisListType


def rwkv_moe_layer(nc, x, Wr, Wk, Wv, Wo, decay, ln_w, wg_red, wg, w1, b1, w2, b2, out):
    P = 128
    B, T, D = x.shape
    E, _, HID = w1.shape
    GD = wg_red.shape[0]
    N = B * T
    TILES = N // P
    GT = 4
    G = TILES // GT
    GC = GT * P
    GPB = T // GC
    HC = HID // P
    NT = TILES + E - 1
    REG = N + P
    PAD = E * REG
    C_MEAN, C_VAR, C_RSTD, C_SCORE, C_ID = D, D + 1, D + 2, D + 3, D + 4
    ROW = D + 5
    LN_EPS, RMS_EPS, GATE_EPS = 1e-5, 1e-6, 1e-4
    NB = 4

    x_v = x.rearrange("b (s p) d -> p (b s) d", p=P)
    out_rows = out.rearrange("b t d -> (b t) d")
    regions = nc.dram_tensor("regions", (PAD + P, ROW), F32).ap()

    ctx = ExitStack()
    with ctx:
        def sb(name, shape, dt=F32):
            return ctx.enter_context(nc.sbuf_tensor(name, shape, dt))

        def pb(name):
            return ctx.enter_context(nc.psum_tensor(name, [P, 512], F32))

        def sem(name):
            return ctx.enter_context(nc.semaphore(name))

        x_all = sb("x_all", [P, TILES, D])
        w1_sb = sb("w1_sb", [P, E * HID])
        w2_sb = sb("w2_sb", [P, E * HID])
        w_nat = sb("w_nat", [P, 4, D])
        wT = sb("wT", [P, 4, D])
        dec_in = sb("dec_in", [P, 1])
        lnw = sb("lnw", [P, 1])
        wgr = sb("wgr", [GD, D])
        wg_sb = sb("wg_sb", [E, GD])
        b1_sp = sb("b1_sp", [P, E * HID // P])
        b2_sp = sb("b2_sp", [E, D])
        b1_part = sb("b1_part", [P, 3, E * HID // P], BF16)
        b2_part = sb("b2_part", [E, 3, D], BF16)
        b1_rows = sb("b1_rows", [3, E * HID], BF16)
        b2_rows = sb("b2_rows", [3, E * HID], BF16)
        ident = sb("ident", [P, P])
        before = sb("before", [P, P], BF16)
        ones_bf = sb("ones_bf", [P, P], BF16)
        mean_w = sb("mean_w", [P, P])
        neg_half = sb("neg_half", [P, TILES])
        half = sb("half", [E, 1])
        ones_col = sb("ones_col", [P, 1])
        zero_row = sb("zero_row", [P, T])
        scale_t = sb("scale_t", [P, T])
        gain = sb("gain", [P, T])
        dec_row = sb("dec_row", [P, T])
        dcol = sb("dcol", [P, 4])
        first_i = sb("first_i", [P, GT, E], I32)
        first_w = sb("first_w", [P, GT, E])
        reg_i = sb("reg_i", [P, GT, E], I32)
        reg_base = sb("reg_base", [P, GT, E])
        ids = sb("ids", [P, TILES], I32)
        pad_row = sb("pad_row", [P, ROW])
        gsq = sb("gsq", [E, GD])
        gn = sb("gn", [E, 4])
        wgu = sb("wgu", [E, GD])
        wguT = sb("wguT", [GD, E])
        gate_m = sb("gate_m", [P, E])
        gate_c = sb("gate_c", [P, E])
        st1 = sb("st1", [P, TILES, 6])
        mv1 = sb("mv1", [P, TILES, 2])
        ve1 = sb("ve1", [P, TILES])
        rstd1 = sb("rstd1", [P, TILES])
        shift1 = sb("shift1", [P, TILES])
        xn = sb("xn", [P, 2, GT, D])
        xnT = sb("xnT", [P, 2, GC])
        rt = sb("rt", [P, 2, GC])
        vg = sb("vg", [P, GC])
        kv = sb("kv", [P, GC])
        state = sb("state", [P, 2, GC])
        y = sb("y", [P, 2, GC])
        y2 = sb("y2", [P, 2, GC])
        ssm = sb("ssm", [P, 2, GT])
        rrms = sb("rrms", [P, 2, GT])
        rows = sb("rows", [P, TILES, ROW])
        st2 = sb("st2", [P, GT, 6])
        ve2 = sb("ve2", [P, 2, GT])
        x1T = sb("x1T", [P, 2, GC])
        lg = sb("lg", [P, GT, E])
        mx = sb("mx", [P, GT])
        dl = sb("dl", [P, 2, GT, E])
        cand = sb("cand", [P, GT, E])
        cmx = sb("cmx", [P, GT])
        oneh = sb("oneh", [P, 2, GT, E], BF16)
        ex = sb("ex", [P, 2, GT, E])
        sx = sb("sx", [P, 2, GT])
        group_n = sb("group_n", [P, 2, E])
        before_n = sb("before_n", [P, G + 1, E], BF16)
        pos_f = sb("pos_f", [P, GT, E])
        pos_m = sb("pos_m", [P, GT, E])
        pos = sb("pos", [P, TILES], I32)
        fill_row = sb("fill_row", [1, E], I32)
        cnt_i = sb("cnt_i", [1, 2, E], I32)
        tl = sb("tl", [1, E])
        tl_end = sb("tl_end", [1, E])
        ones_row = sb("ones_row", [1, E])
        j_i = sb("j_i", [1, NT, E], I32)
        j_f = sb("j_f", [1, NT, E])
        past = sb("past", [1, NT, E])
        past_t = sb("past_t", [1, NT, E])
        exp_j = sb("exp_j", [1, NT])
        skip_j = sb("skip_j", [1, NT])
        row_a = sb("row_a", [1, NT])
        row_b = sb("row_b", [1, NT])
        tab_row = sb("tab_row", [1, NT], I32)
        tab_off = sb("tab_off", [1, NT], I32)
        xs = [sb(f"xs{k}", [P, ROW]) for k in range(NB)]
        tok = [sb(f"tok{k}", [P, 1], I32) for k in range(NB)]
        ob = [sb(f"ob{k}", [P, D]) for k in range(NB)]
        zn = [sb(f"zn{k}", [P, D]) for k in range(2)]
        znT = [sb(f"znT{k}", [P, P]) for k in range(2)]
        h = [sb(f"h{k}", [P, HID]) for k in range(2)]
        hT = [sb(f"hT{k}", [P, HID]) for k in range(2)]

        banks = [pb(f"bank{n}") for n in range(8)]
        T_ps, X_ps, R_ps, K_ps, V_ps, O_ps, S_ps, L_ps = banks
        rank_ps = L_ps[:, GT * E:2 * GT * E]
        up_ps = [R_ps, K_ps]
        hT_ps = [V_ps, O_ps]
        zT_ps = [T_ps, S_ps]
        dn_ps = [L_ps, X_ps]

        X_LOADS = [(0, 1), (1, 2)] + [(g, g + 2) for g in range(2, G, 2)]
        x_loaded = [sem(f"x_loaded{n}") for n in range(len(X_LOADS))]
        names = """params_loaded ffn_loaded brows_loaded pads_stored pad_row_step pad_row_ready
            decay_loaded mats_loaded ident_step ident_ready scale_start consts_step consts_ready decay_step decay_exp
            wT_ps_ready wT_ready gate_step gate_norm gate_pe gain_step gain_ready bias_split
            st1_done mv1_ready ve1_ready rstd1_ready shift1_ready
            xn_ready xnT_ps_ready xnT_ready rkv_ready r_ready vg_ready kv_ready state_ready y_ready y2_ready
            out_ready ssm_ready rrms_ready x1_ready st2_ready mv2_ready ve2_ready rstd2_ready
            x1T_ps_ready x1T_ready logits_ready lg_ready mx_ready dl_ready cand_ready cmx_ready oneh_ready
            ex_ready sx_ready score_ready group_n_ready before_n_ready rank_ready posf_ready posm_ready pos_ready
            ids_ready scattered counts_ready fill_ready tab_step tab_ready
            zn_ready zT_ps_ready zT_ready up_ready h_ready hT_ps_ready hT_ready down_ready ob_ready tok_ready
            """.split()
        s = {n: sem(n) for n in names}
        xs_loaded = [sem(f"xs_loaded{k}") for k in range(NB)]
        stored = [sem(f"stored{k}") for k in range(NB)]

        STEPS = G + 5
        SPLITS = 10
        PARAMS = 16 * 2
        block = ctx.enter_context(nc.Block())

        def pad_tiles(eng, e0, e1):
            _, at = nc.values_load_multi_w_load_instructions(fill_row[0:1, e0:e1], engines=[eng.engine],
                                                             min_val=0, max_val=(E - 1) * REG + N)
            for row in at:
                eng.dma_start(regions[bass.ds(row, P), :], pad_row[:, :]).then_inc(s["pads_stored"], 16)

        @block.sync
        def _(sp):
            for n, (g0, g1) in enumerate(X_LOADS):
                sp.dma_start(x_all[:, GT * g0:GT * g1, :], x_v[:, GT * g0:GT * g1, :]).then_inc(x_loaded[n], 16)
                if n == 1:
                    sp.dma_start(wgr[:, :], wg_red).then_inc(s["params_loaded"], 16)
                    sp.dma_start(wg_sb[:, :], wg).then_inc(s["params_loaded"], 16)
                if n == 2:
                    sp.dma_start(b1_sp[:, :], b1.rearrange("e h -> (e h)").rearrange("(p c) -> p c", p=P)
                                 ).then_inc(s["ffn_loaded"], 16)
                    sp.dma_start(b2_sp[:, :], b2).then_inc(s["ffn_loaded"], 16)
            sp.wait_ge(s["pad_row_ready"], 1)
            sp.dma_start(regions[PAD:PAD + P, :], pad_row[:, :]).then_inc(s["pads_stored"], 16)
            sp.wait_ge(s["bias_split"], SPLITS)
            for n in range(3):
                sp.dma_start(b1_rows[n:n + 1, :], b1_part[:, n, :]).then_inc(s["brows_loaded"], 16)
                sp.dma_start(b2_rows[n:n + 1, :].rearrange("a (e h) -> a e h", e=E)[:, :, 0:D],
                             b2_part[:, n, :]).then_inc(s["brows_loaded"], 16)
            sp.dma_start(w1_sb[:, :].rearrange("p (e h) -> p e h", e=E), w1.rearrange("e d h -> d e h")
                         ).then_inc(s["ffn_loaded"], 16)
            sp.dma_start(w2_sb[:, :].rearrange("p (c d) -> p c d", d=D),
                         w2.rearrange("e h d -> (e h) d").rearrange("(c p) d -> p c d", p=P)
                         ).then_inc(s["ffn_loaded"], 16)

            sp.wait_ge(s["fill_ready"], 1)
            pad_tiles(sp, 0, E // 2)

            sp.wait_ge(s["tab_ready"], 1)
            sp.wait_ge(s["scattered"], 16 * TILES)
            sp.wait_ge(s["pads_stored"], 16 * (1 + E))

            def load(j, k, turn):
                row = sp.value_load(tab_row[0:1, bass.ds(j, 1)], min_val=0, max_val=PAD)
                if turn is not None:
                    sp.wait_ge(s["tok_ready"], j - NB + 1)
                    sp.wait_ge(s["ob_ready"], j - NB + 1)
                sp.dma_start(xs[k][:, :], regions[bass.ds(row, P), :]).then_inc(xs_loaded[k], 16)

            for k in range(NB):
                load(k, k, None)
            with sp.Fori(1, NT // NB) as i:
                for k in range(NB):
                    load(i * NB + k, k, i)
            for j in range(NT // NB * NB, NT):
                load(j, j % NB, j // NB)

        @block.gpsimd
        def _(pool):
            gp = nc.gpsimd
            gp.memset(neg_half[:, :], -0.5)
            gp.memset(half[:, :], 0.5)
            gp.memset(ones_col[:, :], 1.0)
            gp.memset(ones_bf[:, :], 1.0)
            gp.memset(ident[:, :], 0.0).then_inc(s["ident_step"], 1)
            pool.wait_ge(s["ident_step"], 1)
            gp.affine_select(out=ident[:, :], in_=ident[:, :], compare_op=ALU.not_equal, fill=1.0, base=0,
                             pattern=[[-1, P]], channel_multiplier=1).then_inc(s["ident_ready"], 1)
            gp.memset(zero_row[:, :], 0.0)
            gp.memset(scale_t[:, 0:1], 1.0).then_inc(s["scale_start"], 1)

            def rstd1_of(g):
                t0 = GT * g
                pool.wait_ge(s["ve1_ready"], g // 2 + 1)
                gp.tensor_tensor(rstd1[:, t0:t0 + 2 * GT], ve1[:, t0:t0 + 2 * GT], neg_half[:, 0:2 * GT], op=ALU.pow
                                 ).then_inc(s["rstd1_ready"], 1)

            rstd1_of(0)
            pool.wait_ge(s["gate_step"], 2)
            gp.tensor_tensor(gn[:, 1:2], gn[:, 0:1], half[:, :], op=ALU.pow).then_inc(s["gate_norm"], 1)
            gp.memset(pad_row[:, :], 0.0).then_inc(s["pad_row_step"], 1)
            pool.wait_ge(s["pad_row_step"], 1)
            gp.memset(pad_row[:, C_ID:C_ID + 1].bitcast(I32), 1 << 20).then_inc(s["pad_row_ready"], 1)
            gp.affine_select(out=before[:, :], in_=ones_bf[:, :], compare_op=ALU.is_gt, fill=0.0, base=0,
                             pattern=[[1, P]], channel_multiplier=-1)
            gp.memset(mean_w[:, :], 1.0 / D)
            gp.memset(before_n[:, 0, :], 0.0)
            gp.iota(first_i[:, :, :], pattern=[[0, GT], [-1, E]], base=E, channel_multiplier=0)
            gp.iota(reg_i[:, :, :], pattern=[[0, GT], [REG, E]], base=0, channel_multiplier=0)
            gp.iota(j_i[:, :, :], pattern=[[1, NT], [0, E]], base=0, channel_multiplier=0)
            gp.memset(ones_row[:, :], 1.0)
            gp.iota(ids[:, :], pattern=[[P, TILES]], base=0, channel_multiplier=1).then_inc(s["consts_step"], 1)
            pool.wait_ge(s["consts_step"], 1)
            gp.tensor_copy(rows[:, :, C_ID].bitcast(I32), ids[:, :])
            gp.tensor_copy(first_w[:, :, :], first_i[:, :, :])
            gp.tensor_copy(reg_base[:, :, :], reg_i[:, :, :])
            gp.tensor_copy(j_f[:, :, :], j_i[:, :, :]).then_inc(s["consts_ready"], 1)
            pool.wait_ge(s["ffn_loaded"], 32)
            n = 0
            for full, part in ((b1_sp, b1_part), (b2_sp, b2_part)):
                for m in range(3):
                    gp.tensor_copy(part[:, m, :], full[:, :]).then_inc(s["bias_split"], 1)
                    n += 1
                    if m < 2:
                        pool.wait_ge(s["bias_split"], n)
                        gp.tensor_tensor(full[:, :], full[:, :], part[:, m, :], op=ALU.subtract
                                         ).then_inc(s["bias_split"], 1)
                        n += 1
                        pool.wait_ge(s["bias_split"], n)

            def rms(g):
                pool.wait_ge(s["ssm_ready"], g + 1)
                gp.tensor_tensor(rrms[:, g % 2, :], ssm[:, g % 2, :], neg_half[:, 0:GT], op=ALU.pow
                                 ).then_inc(s["rrms_ready"], 1)

            def rstd2_of(g):
                pool.wait_ge(s["ve2_ready"], g + 1)
                gp.tensor_tensor(rows[:, GT * g:GT * g + GT, C_RSTD], ve2[:, g % 2, :], neg_half[:, 0:GT], op=ALU.pow
                                 ).then_inc(s["rstd2_ready"], 1)

            def count(g):
                pool.wait_ge(s["oneh_ready"], g + 1)
                if g >= 1:
                    pool.wait_ge(s["before_n_ready"], g)
                gp.tensor_tensor(group_n[:, :, :], oneh[:, g % 2, 0:2, :], oneh[:, g % 2, 2:4, :], op=ALU.add
                                 ).then_inc(s["group_n_ready"], 1)
                pool.wait_ge(s["group_n_ready"], 2 * g + 1)
                gp.tensor_tensor(group_n[:, 0, :], group_n[:, 0, :], group_n[:, 1, :], op=ALU.add
                                 ).then_inc(s["group_n_ready"], 1)
                pool.wait_ge(s["group_n_ready"], 2 * g + 2)
                gp.tensor_tensor(before_n[:, g + 1, :], before_n[:, g, :], group_n[:, 0, :], op=ALU.add
                                 ).then_inc(s["before_n_ready"], 1)

            def scatter(g):
                pool.wait_ge(s["pos_ready"], g + 1)
                pool.wait_ge(s["score_ready"], g + 1)
                for n in range(GT):
                    t = GT * g + n
                    gp.indirect_dma_start(out=regions, out_offset=bass.IndirectOffsetOnAxis(ap=pos[:, t:t + 1], axis=0),
                                          in_=rows[:, t, :], in_offset=None,
                                          bounds_check=PAD - 1, oob_is_err=False).then_inc(s["scattered"], 16)

            for st in range(STEPS):
                if 0 <= st - 2 < G:
                    rms(st - 2)
                if 0 <= st - 5 < G:
                    scatter(st - 5)
                if 0 <= st - 4 < G - 1:
                    count(st - 4)
                if st - 3 == G - 1:
                    count(G - 1)
                if 0 <= st - 2 < G:
                    rstd2_of(st - 2)
                if 2 * st + 2 < G:
                    rstd1_of(2 * st + 2)

            def token_numbers(j, k, turn):
                pool.wait_ge(xs_loaded[k], turn * 16 + 16)
                if turn > 0:
                    pool.wait_ge(stored[k], turn * 16)
                gp.tensor_copy(tok[k][:, :], xs[k][:, C_ID:C_ID + 1].bitcast(I32)).then_inc(s["tok_ready"], 1)

            def store(j, k, turn):
                pool.wait_ge(s["ob_ready"], j + 1)
                pool.wait_ge(s["tok_ready"], j + 1)
                gp.indirect_dma_start(out=out_rows, out_offset=bass.IndirectOffsetOnAxis(ap=tok[k][:, 0:1], axis=0),
                                      in_=ob[k][:, :], in_offset=None,
                                      bounds_check=N - 1, oob_is_err=False).then_inc(stored[k], 16)

            token_numbers(0, 0, 0)
            for k in range(NB - 1):
                token_numbers(k + 1, k + 1, 0)
                store(k, k, 0)
            for j in range(NB, NT):
                token_numbers(j, j % NB, j // NB)
                store(j - 1, (j - 1) % NB, None)
            store(NT - 1, (NT - 1) % NB, None)
            for k in range(NB):
                pool.wait_ge(stored[k], 16 * len(range(k, NT, NB)))

        @block.scalar
        def _(act):
            ac = nc.scalar
            act.dma_start(dec_in[:, :], decay.rearrange("(p a) -> p a", a=1)).then_inc(s["decay_loaded"], 16)
            for n, w in enumerate((Wr, Wk, Wv, Wo)):
                act.dma_start(w_nat[:, n, :], w).then_inc(s["mats_loaded"], 16)
            act.dma_start(lnw[:, :], ln_w.rearrange("(p a) -> p a", a=1)).then_inc(s["mats_loaded"], 16)
            act.wait_ge(s["decay_loaded"], 16)
            ac.activation(dcol[:, 0:1], dec_in[:, :], ACT.Exp, scale=-1.0).then_inc(s["decay_exp"], 1)

            def normalise(g):
                act.wait_ge(s["shift1_ready"], g // 2 + 1)
                if g >= 2:
                    act.wait_ge(s["xnT_ps_ready"], g - 1)
                for n in range(GT):
                    t = GT * g + n
                    last = ac.activation(xn[:, g % 2, n, :], x_all[:, t, :], ACT.Identity, bias=shift1[:, t:t + 1],
                                         scale=rstd1[:, t:t + 1])
                last.then_inc(s["xn_ready"], 1)

            act.wait_ge(s["wT_ps_ready"], 1)
            act.wait_ge(s["mats_loaded"], 16 * 5)
            ac.copy(wT[:, 0:3, :], X_ps[:, 0:3 * D].rearrange("p (a b) -> p a b", a=3))
            ac.activation(wT[:, 3, :], X_ps[:, 3 * D:4 * D], ACT.Copy, scale=lnw[:, 0:1]).then_inc(s["wT_ready"], 1)
            normalise(0)

            def evac_xn(g):
                act.wait_ge(s["xnT_ps_ready"], g + 1)
                if g >= 2:
                    act.wait_ge(s["rkv_ready"], 2 * (g - 1))
                ac.copy(xnT[:, g % 2, :], T_ps[:, :]).then_inc(s["xnT_ready"], 1)

            def tanh_r(g):
                act.wait_ge(s["rkv_ready"], 2 * g + 2)
                if g >= 2:
                    act.wait_ge(s["y_ready"], g - 1)
                ac.activation(rt[:, g % 2, :], R_ps[:, :], ACT.Tanh, scale=0.5).then_inc(s["r_ready"], 1)

            def squares(g):
                act.wait_ge(s["y_ready"], g + 1)
                if g >= 2:
                    act.wait_ge(s["out_ready"], g - 1)
                ac.activation(y2[:, g % 2, :], y[:, g % 2, :], ACT.Square).then_inc(s["y2_ready"], 1)

            def evac_x1(g):
                act.wait_ge(s["x1T_ps_ready"], g + 1)
                if g >= 2:
                    act.wait_ge(s["logits_ready"], g - 1)
                ac.copy(x1T[:, g % 2, :], X_ps[:, :]).then_inc(s["x1T_ready"], 1)

            def exps(g):
                act.wait_ge(s["dl_ready"], g + 1)
                if g >= 2:
                    act.wait_ge(s["sx_ready"], g - 1)
                ac.activation(ex[:, g % 2, :, :], dl[:, g % 2, :, :], ACT.Exp).then_inc(s["ex_ready"], 1)

            for st in range(STEPS):
                if 0 <= st < G:
                    evac_xn(st)
                if 0 <= st - 3 < G:
                    evac_x1(st - 3)
                if 0 <= st + 1 < G:
                    normalise(st + 1)
                if 0 <= st - 3 < G:
                    exps(st - 3)
                if 0 <= st - 1 < G:
                    squares(st - 1)
                if 0 <= st < G:
                    tanh_r(st)

            act.wait_ge(s["fill_ready"], 1)
            act.wait_ge(s["pad_row_ready"], 1)
            pad_tiles(act, E // 2, E)

            def evac_z(j, k, first):
                act.wait_ge(s["zT_ps_ready"], j + 1)
                if not first:
                    act.wait_ge(s["up_ready"], j - 1)
                ac.copy(znT[k % 2][:, :], zT_ps[k % 2][:, 0:P]).then_inc(s["zT_ready"], 1)

            def gelu(j, k, first):
                act.wait_ge(s["up_ready"], j + 1)
                if not first:
                    act.wait_ge(s["hT_ps_ready"], j - 1)
                ac.activation(h[k % 2][:, :], up_ps[k % 2][:, :], ACT.Gelu).then_inc(s["h_ready"], 1)

            evac_z(0, 0, True)
            gelu(0, 0, True)
            evac_z(1, 1, True)
            gelu(1, 1, True)
            evac_z(2, 0, False)
            loops = (NT - 2) // NB
            with act.Fori(0, loops) as i:
                for k in range(NB):
                    gelu(i * NB + 2 + k, k, False)
                    evac_z(i * NB + 3 + k, 1 + k, False)
            for j in range(loops * NB + 2, NT):
                gelu(j, j, False)
                if j + 1 < NT:
                    evac_z(j + 1, j + 1, False)

        @block.vector
        def _(dve):
            ve = nc.vector
            def stats1_of(g):
                t0 = GT * g
                for n in range(t0, t0 + 2 * GT):
                    for m, (g0, _) in enumerate(X_LOADS):
                        if n == GT * g0:
                            dve.wait_ge(x_loaded[m], 16)
                    last = ve.bn_stats(st1[:, n, :], x_all[:, n, :])
                last.then_inc(s["st1_done"], 1)
                dve.wait_ge(s["st1_done"], g // 2 + 1)
                for n in range(t0, t0 + 2 * GT):
                    last = ve.bn_aggr(mv1[:, n, :], st1[:, n, :])
                last.then_inc(s["mv1_ready"], 1)
                dve.wait_ge(s["mv1_ready"], g // 2 + 1)
                ve.tensor_scalar(ve1[:, t0:t0 + 2 * GT], mv1[:, t0:t0 + 2 * GT, 1], LN_EPS, None, ALU.add
                                 ).then_inc(s["ve1_ready"], 1)

            def shift1_of(g):
                t0 = GT * g
                dve.wait_ge(s["rstd1_ready"], g // 2 + 1)
                ve.scalar_tensor_tensor(shift1[:, t0:t0 + 2 * GT], mv1[:, t0:t0 + 2 * GT, 0], -1.0,
                                        rstd1[:, t0:t0 + 2 * GT], ALU.mult, ALU.mult).then_inc(s["shift1_ready"], 1)

            stats1_of(0)
            dve.wait_ge(s["decay_exp"], 1)
            ve.tensor_scalar(dcol[:, 1:2], dcol[:, 0:1], 1.0, None, ALU.add).then_inc(s["decay_step"], 1)
            dve.wait_ge(s["params_loaded"], PARAMS)
            ve.tensor_tensor(gsq[:, :], wg_sb[:, :], wg_sb[:, :], ALU.mult).then_inc(s["gate_step"], 1)
            dve.wait_ge(s["decay_step"], 1)
            ve.reciprocal(dcol[:, 0:1], dcol[:, 1:2]).then_inc(s["decay_step"], 1)
            dve.wait_ge(s["gate_step"], 1)
            ve.tensor_reduce(gn[:, 0:1], gsq[:, :], AX.X, ALU.add).then_inc(s["gate_step"], 1)
            dve.wait_ge(s["decay_step"], 2)
            ve.tensor_scalar(dcol[:, 2:3], dcol[:, 0:1], 1e-7, None, ALU.max).then_inc(s["decay_step"], 1)
            shift1_of(0)
            ve.memset(state[:, 1, GC - 1:GC], 0.0)
            dve.wait_ge(s["gate_norm"], 1)
            ve.tensor_scalar(gn[:, 2:3], gn[:, 1:2], GATE_EPS, None, ALU.max).then_inc(s["gate_step"], 1)
            dve.wait_ge(s["gate_step"], 3)
            ve.reciprocal(gn[:, 3:4], gn[:, 2:3]).then_inc(s["gate_step"], 1)
            dve.wait_ge(s["gate_step"], 4)
            ve.tensor_scalar(wgu[:, :], wg_sb[:, :], gn[:, 3:4], None, ALU.mult).then_inc(s["gate_step"], 1)

            def decays():
                dve.wait_ge(s["decay_step"], 3)
                dve.wait_ge(s["scale_start"], 1)
                ve.tensor_scalar(dec_row[:, :], zero_row[:, :], dcol[:, 2:3], None, ALU.add
                                 ).then_inc(s["gain_step"], 1)
                dve.wait_ge(s["gain_step"], 1)
                ve.tensor_tensor_scan(scale_t[:, 1:T], dec_row[:, 1:T], zero_row[:, 1:T], 1.0, ALU.mult, ALU.add
                                      ).then_inc(s["gain_step"], 1)
                dve.wait_ge(s["gain_step"], 2)
                ve.tensor_scalar(gain[:, :], scale_t[:, :], 0.5e10, 0.5, ALU.mult, ALU.min)
                ve.memset(dec_row[:, 0:1], 0.0).then_inc(s["gain_ready"], 1)
                dve.wait_ge(s["gain_ready"], 1)

            def gate_matrix():
                dve.wait_ge(s["gate_pe"], 1)
                ve.tensor_copy(wguT[:, :], S_ps[0:GD, 0:E]).then_inc(s["gate_step"], 1)
                dve.wait_ge(s["gate_pe"], 2)
                ve.tensor_copy(gate_m[:, :], L_ps[:, 0:E]).then_inc(s["gate_step"], 1)
                dve.wait_ge(s["gate_pe"], 3)
                dve.wait_ge(s["gate_step"], 7)
                ve.tensor_tensor(gate_c[:, :], gate_m[:, :], O_ps[:, 0:E], ALU.subtract).then_inc(s["gate_step"], 1)
                dve.wait_ge(s["consts_ready"], 1)

            def step(st):
                rec, res, cho, pla = st - 1, st - 2, st - 3, st - 4
                c = rec % GPB * GC
                if 0 <= rec < G:
                    dve.wait_ge(s["rkv_ready"], 2 * rec + 1)
                    ve.tensor_tensor(vg[:, :], V_ps[:, :], gain[:, c:c + GC], ALU.mult).then_inc(s["vg_ready"], 1)
                if 0 <= res < G:
                    dve.wait_ge(s["out_ready"], res + 1)
                    ve.tensor_scalar(ssm[:, res % 2, :], S_ps[:, 0:GT], 1.0 / D, RMS_EPS, ALU.mult, ALU.add
                                     ).then_inc(s["ssm_ready"], 1)
                if 0 <= rec < G:
                    dve.wait_ge(s["rkv_ready"], 2 * rec + 2)
                    dve.wait_ge(s["vg_ready"], rec + 1)
                    ve.tensor_tensor(kv[:, :], K_ps[:, :], vg[:, :], ALU.mult).then_inc(s["kv_ready"], 1)
                if 0 <= pla < G:
                    dve.wait_ge(s["rank_ready"], pla + 1)
                    if cho < G:
                        dve.wait_ge(s["logits_ready"], cho + 1)
                    ve.tensor_tensor(pos_f[:, :, :], rank_ps.rearrange("p (a b) -> p a b", a=GT),
                                     reg_base[:, :, :], ALU.add).then_inc(s["posf_ready"], 1)
                if 0 <= cho < G:
                    dve.wait_ge(s["logits_ready"], cho + 1)
                    dve.wait_ge(s["rstd2_ready"], cho + 1)
                    t0 = GT * cho
                    ve.tensor_tensor(lg[:, :, :], L_ps[:, 0:GT * E].rearrange("p (a b) -> p a b", a=GT),
                                     rows[:, t0:t0 + GT, C_RSTD:C_RSTD + 1].broadcast_to([P, GT, E]),
                                     ALU.mult).then_inc(s["lg_ready"], 1)
                if 0 <= pla < G:
                    dve.wait_ge(s["posf_ready"], pla + 1)
                    ve.tensor_tensor(pos_m[:, :, :], pos_f[:, :, :], oneh[:, pla % 2, :, :], ALU.mult
                                     ).then_inc(s["posm_ready"], 1)
                if 0 <= rec < G:
                    dve.wait_ge(s["kv_ready"], rec + 1)
                    ve.tensor_tensor_scan(state[:, rec % 2, :], dec_row[:, c:c + GC], kv[:, :],
                                          state[:, (rec + 1) % 2, GC - 1:GC], ALU.mult, ALU.add
                                          ).then_inc(s["state_ready"], 1)
                if 0 <= cho < G:
                    dve.wait_ge(s["lg_ready"], cho + 1)
                    ve.tensor_reduce(mx[:, :], lg[:, :, :], AX.X, ALU.max).then_inc(s["mx_ready"], 1)
                    dve.wait_ge(s["mx_ready"], cho + 1)
                    if cho >= 2:
                        dve.wait_ge(s["ex_ready"], cho - 1)
                    ve.tensor_tensor(dl[:, cho % 2, :, :], lg[:, :, :], mx[:, :].unsqueeze(2).broadcast_to([P, GT, E]),
                                     ALU.subtract).then_inc(s["dl_ready"], 1)
                if 0 <= pla < G:
                    dve.wait_ge(s["posm_ready"], pla + 1)
                    with nc.allow_low_precision(reason="whole numbers"):
                        ve.tensor_reduce(pos[:, GT * pla:GT * pla + GT], pos_m[:, :, :], AX.X, ALU.add
                                         ).then_inc(s["pos_ready"], 1)
                if 0 <= rec < G:
                    dve.wait_ge(s["state_ready"], rec + 1)
                    dve.wait_ge(s["r_ready"], rec + 1)
                    if rec >= 2:
                        dve.wait_ge(s["out_ready"], rec - 1)
                        dve.wait_ge(s["y2_ready"], rec - 1)
                    ve.scalar_tensor_tensor(y[:, rec % 2, :], rt[:, rec % 2, :], 1.0, state[:, rec % 2, :],
                                            ALU.add, ALU.mult).then_inc(s["y_ready"], 1)
                if 0 <= cho < G:
                    dve.wait_ge(s["dl_ready"], cho + 1)
                    ve.scalar_tensor_tensor(cand[:, :, :], dl[:, cho % 2, :, :], 0.0, first_w[:, :, :],
                                            ALU.is_equal, ALU.mult).then_inc(s["cand_ready"], 1)
                if 0 <= res < G:
                    dve.wait_ge(s["rrms_ready"], res + 1)
                    for n in range(GT):
                        t = GT * res + n
                        last = ve.scalar_tensor_tensor(rows[:, t, 0:D], O_ps[:, n * D:(n + 1) * D],
                                                       rrms[:, res % 2, n:n + 1], x_all[:, t, :], ALU.mult, ALU.add)
                    last.then_inc(s["x1_ready"], 1)
                if 0 <= cho < G:
                    dve.wait_ge(s["cand_ready"], cho + 1)
                    ve.tensor_reduce(cmx[:, :], cand[:, :, :], AX.X, ALU.max).then_inc(s["cmx_ready"], 1)
                if 0 <= res < G:
                    dve.wait_ge(s["x1_ready"], res + 1)
                    for n in range(GT):
                        last = ve.bn_stats(st2[:, n, :], rows[:, GT * res + n, 0:D])
                    last.then_inc(s["st2_ready"], 1)
                if 0 <= cho < G:
                    dve.wait_ge(s["cmx_ready"], cho + 1)
                    if cho >= 2:
                        dve.wait_ge(s["rank_ready"], cho - 1)
                        dve.wait_ge(s["group_n_ready"], 2 * (cho - 2) + 1)
                    ve.tensor_tensor(oneh[:, cho % 2, :, :], cand[:, :, :],
                                     cmx[:, :].unsqueeze(2).broadcast_to([P, GT, E]), ALU.is_equal
                                     ).then_inc(s["oneh_ready"], 1)
                if 0 <= res < G:
                    dve.wait_ge(s["st2_ready"], res + 1)
                    for n in range(GT):
                        last = ve.bn_aggr(rows[:, GT * res + n, C_MEAN:C_MEAN + 2], st2[:, n, :])
                    last.then_inc(s["mv2_ready"], 1)
                if 0 <= cho < G:
                    dve.wait_ge(s["ex_ready"], cho + 1)
                    ve.tensor_reduce(sx[:, cho % 2, :], ex[:, cho % 2, :, :], AX.X, ALU.add).then_inc(s["sx_ready"], 1)
                if 0 <= res < G:
                    dve.wait_ge(s["mv2_ready"], res + 1)
                    ve.tensor_scalar(ve2[:, res % 2, :], rows[:, GT * res:GT * res + GT, C_VAR], LN_EPS, None, ALU.add
                                     ).then_inc(s["ve2_ready"], 1)
                if 0 <= cho < G:
                    dve.wait_ge(s["sx_ready"], cho + 1)
                    ve.reciprocal(rows[:, GT * cho:GT * cho + GT, C_SCORE], sx[:, cho % 2, :]
                                  ).then_inc(s["score_ready"], 1)

            for st in range(STEPS - 1):
                if st == 0:
                    decays()
                step(st)
                if 2 * st + 2 < G:
                    stats1_of(2 * st + 2)
                if st == 1:
                    gate_matrix()
                if 2 * st + 2 < G:
                    shift1_of(2 * st + 2)

            dve.wait_ge(s["counts_ready"], 1)
            with nc.allow_low_precision(reason="whole numbers"):
                ve.tensor_tensor(fill_row[:, :], L_ps[0:1, 0:E], reg_base[0:1, 0, :], ALU.add
                                 ).then_inc(s["fill_ready"], 1)
                ve.tensor_scalar(cnt_i[0:1, 0, :], L_ps[0:1, 0:E], float(P - 1), None, ALU.add
                                 ).then_inc(s["tab_step"], 1)
                dve.wait_ge(s["tab_step"], 1)
                ve.tensor_scalar(cnt_i[0:1, 1, :], cnt_i[0:1, 0, :], 7, None, ALU.arith_shift_right
                                 ).then_inc(s["tab_step"], 1)
            dve.wait_ge(s["tab_step"], 2)
            ve.tensor_copy(tl[:, :], cnt_i[0:1, 1, :]).then_inc(s["tab_step"], 1)
            dve.wait_ge(s["tab_step"], 3)
            ve.tensor_tensor_scan(tl_end[:, :], ones_row[:, :], tl[:, :], 0.0, ALU.mult, ALU.add
                                  ).then_inc(s["tab_step"], 1)
            dve.wait_ge(s["tab_step"], 4)
            ve.tensor_tensor(past[:, :, :], j_f[:, :, :], tl_end[:, :].unsqueeze(1).broadcast_to([1, NT, E]),
                             ALU.is_ge).then_inc(s["tab_step"], 1)
            dve.wait_ge(s["tab_step"], 5)
            ve.tensor_tensor(past_t[:, :, :], past[:, :, :], tl[:, :].unsqueeze(1).broadcast_to([1, NT, E]),
                             ALU.mult)
            ve.tensor_reduce(exp_j[:, :], past[:, :, :], AX.X, ALU.add).then_inc(s["tab_step"], 1)
            dve.wait_ge(s["tab_step"], 6)
            ve.tensor_reduce(skip_j[:, :], past_t[:, :, :], AX.X, ALU.add).then_inc(s["tab_step"], 1)
            dve.wait_ge(s["tab_step"], 7)
            ve.tensor_tensor(row_a[:, :], j_f[:, :, 0], skip_j[:, :], ALU.subtract)
            ve.tensor_scalar(row_b[:, :], exp_j[:, :], float(REG), None, ALU.mult).then_inc(s["tab_step"], 1)
            dve.wait_ge(s["tab_step"], 8)
            ve.scalar_tensor_tensor(row_b[:, :], row_a[:, :], float(P), row_b[:, :], ALU.mult, ALU.add
                                    ).then_inc(s["tab_step"], 1)
            dve.wait_ge(s["tab_step"], 9)
            with nc.allow_low_precision(reason="whole numbers"):
                ve.tensor_scalar(tab_off[:, :], exp_j[:, :], float(E - 1), float(HID), ALU.min, ALU.mult)
                ve.tensor_scalar(tab_row[:, :], row_b[:, :], float(PAD), None, ALU.min).then_inc(s["tab_ready"], 1)

            def norm_z(j, k, turn, first):
                dve.wait_ge(xs_loaded[k], turn * 16 + 16)
                if not first:
                    dve.wait_ge(s["zT_ps_ready"], j - 1)
                ve.tensor_scalar(zn[k % 2][:, :], xs[k][:, 0:D], xs[k][:, C_MEAN:C_MEAN + 1],
                                 xs[k][:, C_RSTD:C_RSTD + 1], ALU.subtract, ALU.mult).then_inc(s["zn_ready"], 1)

            def evac_h(j, k, first):
                dve.wait_ge(s["hT_ps_ready"], j + 1)
                if not first:
                    dve.wait_ge(s["down_ready"], j - 1)
                ve.tensor_copy(hT[k % 2][:, :], hT_ps[k % 2][:, :]).then_inc(s["hT_ready"], 1)

            def finish(j, k, turn, first):
                dve.wait_ge(s["down_ready"], j + 1)
                if not first:
                    dve.wait_ge(stored[k], turn * 16)
                ve.scalar_tensor_tensor(ob[k][:, :], dn_ps[k % 2][:, 0:D], xs[k][:, C_SCORE:C_SCORE + 1],
                                        xs[k][:, 0:D], ALU.mult, ALU.add).then_inc(s["ob_ready"], 1)

            norm_z(0, 0, 0, True)
            norm_z(1, 1, 0, True)
            for j in range(NB + 1):
                evac_h(j, j, j < 2)
                norm_z(j + 2, (j + 2) % NB, (j + 2) // NB, False)
                if j >= 1:
                    finish(j - 1, j - 1, 0, True)
            loops = (NT - 3) // NB
            with dve.Fori(1, loops) as i:
                for k in range(NB):
                    j = i * NB + 1 + k
                    evac_h(j, 1 + k, False)
                    norm_z(j + 2, (3 + k) % NB, i + (3 + k) // NB, False)
                    finish(j - 1, k, i, False)
            for j in range(loops * NB + 1, NT):
                evac_h(j, j, False)
                if j + 2 < NT:
                    norm_z(j + 2, (j + 2) % NB, (j + 2) // NB, False)
                finish(j - 1, (j - 1) % NB, (j - 1) // NB, False)
            finish(NT - 1, (NT - 1) % NB, (NT - 1) // NB, False)

        @block.tensor
        def _(pe):
            te = nc.tensor
            pe.wait_ge(s["mats_loaded"], 16 * 5)
            pe.wait_ge(s["ident_ready"], 1)
            for n in range(4):
                last = te.transpose(X_ps[:, n * D:(n + 1) * D], w_nat[:, n, :], ident[:, :])
            last.then_inc(s["wT_ps_ready"], 1)

            def gate_matrix():
                pe.wait_ge(s["gate_step"], 5)
                te.transpose(S_ps[0:GD, 0:E], wgu[:, :], ident[0:E, 0:E]).then_inc(s["gate_pe"], 1)
                pe.wait_ge(s["gate_step"], 6)
                pe.wait_ge(s["params_loaded"], PARAMS)
                te.matmul(L_ps[:, 0:E], wgr[:, :], wguT[:, :], start=True, stop=True).then_inc(s["gate_pe"], 1)
                pe.wait_ge(s["gate_step"], 7)
                pe.wait_ge(s["consts_ready"], 1)
                te.matmul(O_ps[:, 0:E], mean_w[:, :], gate_m[:, :], start=True, stop=True).then_inc(s["gate_pe"], 1)
                pe.wait_ge(s["gate_step"], 8)

            def project_out(g):
                pe.wait_ge(s["y_ready"], g + 1)
                pe.wait_ge(s["y2_ready"], g + 1)
                if g >= 1:
                    pe.wait_ge(s["x1_ready"], g)
                for n in range(GT):
                    te.matmul(S_ps[:, n:n + 1], y2[:, g % 2, n * P:(n + 1) * P], ones_col[:, :], start=True, stop=True)
                for n in range(GT):
                    last = te.matmul(O_ps[:, n * D:(n + 1) * D], y[:, g % 2, n * P:(n + 1) * P], wT[:, 3, :],
                                     start=True, stop=True)
                last.then_inc(s["out_ready"], 1)

            def turn_xn(g):
                pe.wait_ge(s["xn_ready"], g + 1)
                if g >= 1:
                    pe.wait_ge(s["xnT_ready"], g)
                for n in range(GT):
                    last = te.transpose(T_ps[:, n * P:(n + 1) * P], xn[:, g % 2, n, :], ident[:, :])
                last.then_inc(s["xnT_ps_ready"], 1)

            def project_in(g):
                pe.wait_ge(s["xnT_ready"], g + 1)
                if g >= 1:
                    pe.wait_ge(s["vg_ready"], g)
                te.matmul(V_ps[:, :], wT[:, 2, :], xnT[:, g % 2, :], start=True, stop=True)
                if g >= 1:
                    pe.wait_ge(s["kv_ready"], g)
                te.matmul(K_ps[:, :], wT[:, 1, :], xnT[:, g % 2, :], start=True, stop=True
                          ).then_inc(s["rkv_ready"], 1)
                if g >= 1:
                    pe.wait_ge(s["r_ready"], g)
                te.matmul(R_ps[:, :], wT[:, 0, :], xnT[:, g % 2, :], start=True, stop=True
                          ).then_inc(s["rkv_ready"], 1)

            def turn_x1(g):
                pe.wait_ge(s["x1_ready"], g + 1)
                if g >= 1:
                    pe.wait_ge(s["x1T_ready"], g)
                for n in range(GT):
                    last = te.transpose(X_ps[:, n * P:(n + 1) * P], rows[:, GT * g + n, 0:D], ident[:, :])
                last.then_inc(s["x1T_ps_ready"], 1)

            def ranks(g):
                pe.wait_ge(s["oneh_ready"], g + 1)
                if g >= 1:
                    pe.wait_ge(s["before_n_ready"], g)
                    pe.wait_ge(s["posf_ready"], g)
                pe.wait_ge(s["lg_ready"], g + 1)
                te.matmul(rank_ps, before[:, :], oneh[:, g % 2, :, :].rearrange("p a b -> p (a b)"),
                          start=True, stop=False)
                te.matmul(rank_ps.rearrange("p (a b) -> p a b", a=GT), ones_bf[:, :],
                          before_n[:, g, :].unsqueeze(1).broadcast_to([P, GT, E]), start=False, stop=False)
                for n in range(GT - 1):
                    last = te.matmul(rank_ps.rearrange("p (a b) -> p a b", a=GT)[:, n + 1:GT, :], ones_bf[:, :],
                                     oneh[:, g % 2, n, :].unsqueeze(1).broadcast_to([P, GT - 1 - n, E]),
                                     start=False, stop=(n == GT - 2))
                last.then_inc(s["rank_ready"], 1)

            def logits(g):
                pe.wait_ge(s["x1T_ready"], g + 1)
                if g >= 1:
                    pe.wait_ge(s["lg_ready"], g)
                if g >= 2:
                    pe.wait_ge(s["posf_ready"], g - 1)
                for n in range(GT):
                    last = te.matmul(L_ps[:, n * E:(n + 1) * E], x1T[:, g % 2, n * P:(n + 1) * P], gate_c[:, :],
                                     start=True, stop=True)
                last.then_inc(s["logits_ready"], 1)

            for st in range(STEPS - 1):
                if st == 0:
                    turn_xn(0)
                    pe.wait_ge(s["wT_ready"], 1)
                if 1 <= st < G:
                    turn_xn(st)
                if 0 <= st - 3 < G:
                    turn_x1(st - 3)
                if 0 <= st - 2 < G:
                    project_out(st - 2)
                if 0 <= st - 4 < G:
                    ranks(st - 4)
                if 0 <= st - 3 < G:
                    logits(st - 3)
                if 0 <= st < G:
                    project_in(st)
                if st == 1:
                    gate_matrix()
            pe.wait_ge(s["before_n_ready"], G)
            pe.wait_ge(s["posf_ready"], G)
            te.matmul(L_ps[:, 0:E], ones_bf[:, :], before_n[:, G, :], start=True, stop=True
                      ).then_inc(s["counts_ready"], 1)

            pe.wait_ge(s["tab_ready"], 1)
            pe.wait_ge(s["ffn_loaded"], 16 * 4)
            pe.wait_ge(s["brows_loaded"], 16 * 6)

            def expert_of(j):
                return pe.value_load(tab_off[0:1, bass.ds(j, 1)], min_val=0, max_val=(E - 1) * HID)

            def turn_z(j, k):
                pe.wait_ge(s["zn_ready"], j + 1)
                te.transpose(zT_ps[k % 2][:, 0:P], zn[k % 2][:, :], ident[:, :]).then_inc(s["zT_ps_ready"], 1)

            def up(j, k, first):
                off = expert_of(j)
                pe.wait_ge(s["zT_ready"], j + 1)
                te.matmul(up_ps[k % 2][:, :], ones_bf[0:3, :], b1_rows[:, bass.ds(off, HID)], start=True, stop=False)
                te.matmul(up_ps[k % 2][:, :], znT[k % 2][:, :], w1_sb[:, bass.ds(off, HID)], start=False, stop=True
                          ).then_inc(s["up_ready"], 1)

            def turn_h(j, k):
                pe.wait_ge(s["h_ready"], j + 1)
                for c in range(HC):
                    last = te.transpose(hT_ps[k % 2][:, c * P:(c + 1) * P], h[k % 2][:, c * P:(c + 1) * P], ident[:, :])
                last.then_inc(s["hT_ps_ready"], 1)

            def down(j, k, first):
                off = expert_of(j)
                pe.wait_ge(s["hT_ready"], j + 1)
                if not first:
                    pe.wait_ge(s["ob_ready"], j - 1)
                te.matmul(dn_ps[k % 2][:, 0:D], ones_bf[0:3, :], b2_rows[:, bass.ds(off, D)], start=True, stop=False)
                for c in range(HC):
                    last = te.matmul(dn_ps[k % 2][:, 0:D], hT[k % 2][:, c * P:(c + 1) * P],
                                     w2_sb[:, bass.ds(off + c * D, D)], start=False, stop=(c == HC - 1))
                last.then_inc(s["down_ready"], 1)

            turn_z(0, 0)
            up(0, 0, True)
            turn_z(1, 1)
            for j in range(1, 3):
                turn_h(j - 1, j - 1)
                up(j, j, True)
                down(j - 1, j - 1, True)
                turn_z(j + 1, j + 1)
            PE_TILES = 2 * NB
            loops = (NT - 4) // PE_TILES
            with pe.Fori(0, loops) as i:
                for k in range(3, 3 + PE_TILES):
                    j = i * PE_TILES + k
                    turn_h(j - 1, k - 1)
                    up(j, k, False)
                    down(j - 1, k - 1, False)
                    turn_z(j + 1, k + 1)
            for j in range(loops * PE_TILES + 3, NT + 1):
                turn_h(j - 1, j - 1)
                if j < NT:
                    up(j, j, False)
                down(j - 1, j - 1, False)
                if j + 1 < NT:
                    turn_z(j + 1, j + 1)


_INS = ['L0_attn_x', 'L0_attn_Wr', 'L0_attn_Wk', 'L0_attn_Wv', 'L0_attn_Wo', 'L0_attn_decay', 'L0_attn_ln_w',
        'L0_ffn_wg_red', 'L0_ffn_wg', 'L0_ffn_w1', 'L0_ffn_b1', 'L0_ffn_w2', 'L0_ffn_b2']


def kernel(**inputs):
    import numpy as _np
    import concourse.bacc as _bacc
    from concourse import mybir as _mybir
    from concourse.bass_utils import run_bass_kernel_spmd as _run

    nc = _bacc.Bacc("TRN2", target_bir_lowering=False, num_devices=1)
    arrays, args = {}, []
    for name in _INS:
        a = _np.ascontiguousarray(inputs[name])
        arrays[f"in_{name}_dram"] = a
        args.append(nc.dram_tensor(f"in_{name}_dram", a.shape, _mybir.dt.from_np(a.dtype), kind="ExternalInput").ap())
    shape = inputs['L0_attn_x'].shape
    args.append(nc.dram_tensor("out_0_dram", shape, _mybir.dt.float32, kind="ExternalOutput").ap())
    rwkv_moe_layer(nc, *args)
    r = _run(nc, [arrays], core_ids=[0])
    return r.results[0]["out_0_dram"]
```

```python
import concourse.bass as bass
from concourse import mybir
from contextlib import ExitStack

F32 = mybir.dt.float32
BF16 = mybir.dt.bfloat16
I32 = mybir.dt.int32
ALU = mybir.AluOpType
ACT = mybir.ActivationFunctionType
AX = mybir.AxisListType


def rwkv_moe_layer(nc, x, Wr, Wk, Wv, Wo, decay, ln_w, wg_red, wg, w1, b1, w2, b2, out):
    P = 128
    B, T, D = x.shape
    E, _, HID = w1.shape
    GD = wg_red.shape[0]
    N = B * T
    TILES = N // P
    GT = 4
    G = TILES // GT
    GC = GT * P
    GPB = T // GC
    HC = HID // P
    NT = TILES + E - 1
    GA = G - 2
    NA = -(-(GC * GA - E * (P - 1)) // P)
    REG = N + P
    PAD = E * REG
    C_MEAN, C_VAR, C_RSTD, C_SCORE, C_ID = D, D + 1, D + 2, D + 3, D + 4
    ROW = D + 5
    LN_EPS, RMS_EPS, GATE_EPS = 1e-5, 1e-6, 1e-4
    NB = 8
    LOOP_TILES = NB
    assert REG % P == 0 and REG // P * (E - 1) < 256

    x_v = x.rearrange("b (s p) d -> p (b s) d", p=P)
    out_rows = out.rearrange("b t d -> (b t) d")
    regions = nc.dram_tensor("regions", (PAD + P, ROW), F32).ap()

    ctx = ExitStack()
    with ctx:
        def sb(name, shape, dt=F32):
            return ctx.enter_context(nc.sbuf_tensor(name, shape, dt))

        def pb(name):
            return ctx.enter_context(nc.psum_tensor(name, [P, 512], F32))

        def sem(name):
            return ctx.enter_context(nc.semaphore(name))

        x_all = sb("x_all", [P, TILES, D])
        w1_sb = sb("w1_sb", [P, E * HID])
        w2_sb = sb("w2_sb", [P, E * HID])
        w_nat = sb("w_nat", [P, 4, D])
        wT = sb("wT", [P, 4, D])
        dec_in = sb("dec_in", [P, 1])
        lnw = sb("lnw", [P, 1])
        wgr = sb("wgr", [GD, D])
        wg_sb = sb("wg_sb", [E, GD])
        b1_nat = sb("b1_nat", [E * HC, P])
        BIAS = HC + D
        biases = sb("biases", [P, E * BIAS])
        ident = sb("ident", [P, P])
        before = sb("before", [P, P], BF16)
        ones_bf = sb("ones_bf", [P, P], BF16)
        mean_w = sb("mean_w", [P, P])
        neg_half = sb("neg_half", [P, TILES])
        half = sb("half", [E, 1])
        ones_col = sb("ones_col", [P, 1])
        ssm = sb("ssm", [P, 2, GT])
        zero_row = sb("zero_row", [P, T])
        scale_t = sb("scale_t", [P, T])
        gain = sb("gain", [P, T])
        dec_row = sb("dec_row", [P, T])
        dcol = sb("dcol", [P, 3])
        warm = sb("warm", [P, 2])
        first_i = sb("first_i", [P, GT, E], I32)
        first_w = sb("first_w", [P, GT, E])
        reg_i = sb("reg_i", [1, GT, E], I32)
        reg_base = sb("reg_base", [1, E])
        reg_part = sb("reg_part", [1, GT, E], BF16)
        ids = sb("ids", [P, TILES], I32)
        pad_row = sb("pad_row", [P, ROW])
        gsq = sb("gsq", [E, GD])
        gn = sb("gn", [E, 4])
        wgu = sb("wgu", [E, GD])
        wguT = sb("wguT", [GD, E])
        gate_m = sb("gate_m", [P, E])
        gate_c = sb("gate_c", [P, E])
        st1 = sb("st1", [P, TILES, 6])
        mv1 = sb("mv1", [P, TILES, 2])
        ve1 = sb("ve1", [P, TILES])
        rstd1 = sb("rstd1", [P, TILES])
        shift1 = sb("shift1", [P, TILES])
        xn = sb("xn", [P, 2, GT, D])
        xnT = sb("xnT", [P, 2, GC])
        rt = sb("rt", [P, 2, GC])
        vg = sb("vg", [P, GC])
        kv = sb("kv", [P, GC])
        state = sb("state", [P, 2, GC])
        y = sb("y", [P, 2, GC])
        y2 = sb("y2", [P, 2, GC])
        rrms = sb("rrms", [P, 2, GT])
        rows = sb("rows", [P, TILES, ROW])
        st2 = sb("st2", [P, GT, 6])
        ve2 = sb("ve2", [P, 2, GT])
        x1T = sb("x1T", [P, 2, GC])
        lg = sb("lg", [P, GT, E])
        mx = sb("mx", [P, GT])
        dl = sb("dl", [P, 2, GT, E])
        cand = sb("cand", [P, GT, E])
        cmx = sb("cmx", [P, GT])
        oneh = sb("oneh", [P, 2, GT, E], BF16)
        ex = sb("ex", [P, 2, GT, E])
        sx = sb("sx", [P, 2, GT])
        group_n = sb("group_n", [P, G, E], BF16)
        pos_m = sb("pos_m", [P, GT, E])
        pos = sb("pos", [P, TILES], I32)
        fill_row = sb("fill_row", [1, E], I32)
        cnt_i = sb("cnt_i", [1, 2, E], I32)
        taken = sb("taken", [1, E + 1])
        room = sb("room", [1, 2, E])
        weight = sb("weight", [1, E])
        tl = sb("tl", [1, E])
        tl_end = sb("tl_end", [1, E])
        ones_row = sb("ones_row", [1, E])
        j_i = sb("j_i", [1, NT, E], I32)
        j_f = sb("j_f", [1, NT, E])
        past = sb("past", [1, NT, E])
        past_t = sb("past_t", [1, NT, E])
        exp_j = sb("exp_j", [1, NT])
        skip_j = sb("skip_j", [1, NT])
        row_a = sb("row_a", [1, NT])
        row_b = sb("row_b", [1, NT])
        tab_row = sb("tab_row", [1, NT], I32)
        tab_off = sb("tab_off", [1, NT], I32)
        tab_bias = sb("tab_bias", [1, NT], I32)
        xs = [sb(f"xs{k}", [P, ROW]) for k in range(NB)]
        tok = [sb(f"tok{k}", [P, 1], I32) for k in range(NB)]
        ob = [sb(f"ob{k}", [P, D]) for k in range(NB)]
        yb = [sb(f"yb{k}", [P, D]) for k in range(2)]
        zn = [sb(f"zn{k}", [P, D]) for k in range(2)]
        znT = [sb(f"znT{k}", [P, P]) for k in range(2)]
        w1_cur = [sb(f"w1_cur{k}", [P, HID]) for k in range(2)]
        hb = [sb(f"hb{k}", [P, HID]) for k in range(2)]
        hT = [sb(f"hT{k}", [P, HID]) for k in range(2)]

        banks = [pb(f"bank{n}") for n in range(8)]
        T_ps, X_ps, R_ps, K_ps, V_ps, O_ps, S_ps, L_ps = banks
        rank_ps = S_ps[:, GT * E:2 * GT * E]
        up_ps = [R_ps, K_ps]
        zT_ps = [T_ps, S_ps]
        dn_ps = [L_ps, X_ps]

        X_LOADS = [(g, g + 1) for g in range(4)] + [(g, g + 2) for g in range(4, G, 2)]
        x_loaded = [sem(f"x_loaded{n}") for n in range(len(X_LOADS))]

        def load_of(g):
            return [n for n, (g0, g1) in enumerate(X_LOADS) if g0 <= g < g1][0]

        names = """params_loaded ffn_loaded pads_stored pad_row_step pad_row_ready
            decay_loaded mats_loaded wo_loaded ident_step ident_ready scale_start
            consts_step consts_ready numbers_ready decay_step decay_exp
            wT_ps_ready wT_ready woT_ps_ready woT_ready gate_step gate_norm gate_pe gain_step gain_ready
            st1_done mv1_ready ve1_ready rstd1_ready shift1_ready
            xn_ready xnT_ps_ready xnT_ready rkv_ready r_ready vg_ready kv_ready state_ready y_ready y2_ready
            out_ready ssm_ready rrms_ready x1_ready st2_ready mv2_ready ve2_ready rstd2_ready
            x1T_ps_ready x1T_ready logits_ready lg_ready mx_ready dl_ready cand_ready cmx_ready oneh_ready
            ex_ready sx_ready score_ready group_n_ready rank_ready posm_ready pos_ready
            early_scattered late_scattered counts_ready fill_ready tab_step tab_ready
            b1T_ps_ready b1T_ready w1_ready
            zn_ready zT_ps_ready zT_ready up_ready hb_ready hT_ready down_ready yb_ready ob_ready tok_ready
            """.split()
        s = {n: sem(n) for n in names}
        xs_loaded = [sem(f"xs_loaded{k}") for k in range(NB)]
        stored = [sem(f"stored{k}") for k in range(NB)]

        STEPS = G + 4
        PARAMS = 16 * 2
        STATS_AT = {0: [2], 1: [3], 2: [4], 4: [5]}
        block = ctx.enter_context(nc.Block())

        IN_RANGE = "counts and expert numbers are bounded by the shapes and clamped where the tables are made"

        def table(eng, tab, j0, n, most):
            return nc.values_load_multi_w_load_instructions(tab[0:1, bass.ds(j0, n)], engines=[eng.engine],
                                                            min_val=0, max_val=most,
                                                            skip_runtime_bounds_check_because=IN_RANGE)[1]

        @block.sync
        def _(sp):
            def load_x(n):
                g0, g1 = X_LOADS[n]
                sp.dma_start(x_all[:, GT * g0:GT * g1, :], x_v[:, GT * g0:GT * g1, :]).then_inc(x_loaded[n], 16)

            load_x(0)
            load_x(1)
            for n, w in enumerate((Wr, Wk, Wv)):
                sp.dma_start(w_nat[:, n, :], w).then_inc(s["mats_loaded"], 16)
            sp.dma_start(wg_sb[:, :], wg).then_inc(s["params_loaded"], 16)
            sp.dma_start(wgr[:, :], wg_red).then_inc(s["params_loaded"], 16)
            load_x(2)
            sp.dma_start(w_nat[:, 3, :], Wo).then_inc(s["wo_loaded"], 16)
            sp.dma_start(lnw[:, :], ln_w.rearrange("(p a) -> p a", a=1)).then_inc(s["wo_loaded"], 16)
            for n in range(3, len(X_LOADS)):
                load_x(n)
            sp.dma_start(b1_nat[:, :], b1.rearrange("e (c p) -> (e c) p", p=P)).then_inc(s["ffn_loaded"], 16)
            sp.dma_start(biases[:, :].rearrange("p (e c) -> p e c", e=E)[:, :, HC:BIAS],
                         b2.unsqueeze(0).broadcast_to([P, E, D])).then_inc(s["ffn_loaded"], 16)
            sp.wait_ge(s["pad_row_ready"], 1)
            sp.dma_start(regions[PAD:PAD + P, :], pad_row[:, :]).then_inc(s["pads_stored"], 16)
            sp.wait_ge(s["y_ready"], 1)
            sp.dma_start(w1_sb[:, :].rearrange("p (e h) -> p e h", e=E), w1.rearrange("e d h -> d e h")
                         ).then_inc(s["ffn_loaded"], 16)
            sp.dma_start(w2_sb[:, :].rearrange("p (c d) -> p c d", d=D),
                         w2.rearrange("e h d -> (e h) d").rearrange("(c p) d -> p c d", p=P)
                         ).then_inc(s["ffn_loaded"], 16)

            sp.wait_ge(s["tab_ready"], 1)
            rows_at = table(sp, tab_row, 0, NB, PAD)
            sp.wait_ge(s["early_scattered"], 16 * GT * GA)

            def load(j, k, row, turn):
                if turn is not None:
                    sp.wait_ge(s["tok_ready"], j - NB + 1)
                    sp.wait_ge(s["ob_ready"], j - NB + 1)
                sp.dma_start(xs[k][:, :], regions[bass.ds(row, P), :]).then_inc(xs_loaded[k], 16)

            for k in range(NB):
                load(k, k, rows_at[k], None)
            sp.wait_ge(s["fill_ready"], 1)
            for row in table(sp, fill_row, 0, E, (E - 1) * REG + N):
                sp.dma_start(regions[bass.ds(row, P), :], pad_row[:, :]).then_inc(s["pads_stored"], 16)
            sp.wait_ge(s["tab_ready"], 2)
            sp.wait_ge(s["late_scattered"], 16 * GT * (G - GA))
            sp.wait_ge(s["pads_stored"], 16 * (1 + E))
            loops = (NT - NB) // LOOP_TILES
            with sp.Fori(0, loops) as i:
                rows_at = table(sp, tab_row, i * LOOP_TILES + NB, LOOP_TILES, PAD)
                for k in range(LOOP_TILES):
                    load(i * LOOP_TILES + NB + k, k % NB, rows_at[k], i)
            last_tiles = loops * LOOP_TILES + NB
            rows_at = table(sp, tab_row, last_tiles, NT - last_tiles, PAD)
            for j in range(last_tiles, NT):
                load(j, j % NB, rows_at[j - last_tiles], j // NB)

        @block.gpsimd
        def _(pool):
            gp = nc.gpsimd
            gp.memset(neg_half[:, :], -0.5)
            gp.memset(half[:, :], 0.5)
            gp.memset(ones_col[:, :], 1.0)
            gp.memset(ones_bf[:, :], 1.0)
            gp.memset(ident[:, :], 0.0).then_inc(s["ident_step"], 1)
            pool.wait_ge(s["ident_step"], 1)
            gp.affine_select(out=ident[:, :], in_=ident[:, :], compare_op=ALU.not_equal, fill=1.0, base=0,
                             pattern=[[-1, P]], channel_multiplier=1).then_inc(s["ident_ready"], 1)
            gp.memset(zero_row[:, :], 0.0)
            gp.memset(scale_t[:, 0:1], 1.0).then_inc(s["scale_start"], 1)

            gp.affine_select(out=before[:, :], in_=ones_bf[:, :], compare_op=ALU.is_gt, fill=0.0, base=0,
                             pattern=[[1, P]], channel_multiplier=-1)
            gp.memset(mean_w[:, :], 1.0 / D)
            gp.iota(first_i[:, :, :], pattern=[[0, GT], [-1, E]], base=E, channel_multiplier=0)
            gp.iota(reg_i[:, :, :], pattern=[[0, GT], [REG, E]], base=0, channel_multiplier=0)
            gp.iota(ids[:, :], pattern=[[P, TILES]], base=0, channel_multiplier=1).then_inc(s["consts_step"], 1)
            pool.wait_ge(s["consts_step"], 1)
            gp.tensor_copy(rows[:, :, C_ID].bitcast(I32), ids[:, :])
            gp.tensor_copy(first_w[:, :, :], first_i[:, :, :])
            gp.tensor_copy(reg_part[:, :, :], reg_i[:, :, :])
            gp.tensor_copy(reg_base[:, :], reg_i[:, 0, :]).then_inc(s["consts_ready"], 1)

            def rstd1_of(m):
                t0, t1 = GT * X_LOADS[m][0], GT * X_LOADS[m][1]
                pool.wait_ge(s["ve1_ready"], m + 1)
                gp.tensor_tensor(rstd1[:, t0:t1], ve1[:, t0:t1], neg_half[:, 0:t1 - t0], op=ALU.pow
                                 ).then_inc(s["rstd1_ready"], 1)

            rstd1_of(0)
            rstd1_of(1)
            gp.memset(pad_row[:, :], 0.0).then_inc(s["pad_row_step"], 1)
            gp.memset(ones_row[:, :], 1.0)
            gp.iota(j_i[:, :, :], pattern=[[1, NT], [0, E]], base=0, channel_multiplier=0
                    ).then_inc(s["consts_step"], 1)
            pool.wait_ge(s["pad_row_step"], 1)
            gp.memset(pad_row[:, C_ID:C_ID + 1].bitcast(I32), 1 << 20).then_inc(s["pad_row_ready"], 1)
            pool.wait_ge(s["gate_step"], 2)
            gp.tensor_tensor(gn[:, 1:2], gn[:, 0:1], half[:, :], op=ALU.pow).then_inc(s["gate_norm"], 1)

            def tile_numbers():
                pool.wait_ge(s["consts_step"], 2)
                gp.tensor_copy(j_f[:, :, :], j_i[:, :, :]).then_inc(s["numbers_ready"], 1)

            def rms(g):
                pool.wait_ge(s["ssm_ready"], g + 1)
                gp.tensor_tensor(rrms[:, g % 2, :], ssm[:, g % 2, :], neg_half[:, 0:GT], op=ALU.pow
                                 ).then_inc(s["rrms_ready"], 1)

            def rstd2_of(g):
                pool.wait_ge(s["ve2_ready"], g + 1)
                gp.tensor_tensor(rows[:, GT * g:GT * g + GT, C_RSTD], ve2[:, g % 2, :], neg_half[:, 0:GT], op=ALU.pow
                                 ).then_inc(s["rstd2_ready"], 1)

            def scatter(g):
                pool.wait_ge(s["pos_ready"], g + 1)
                pool.wait_ge(s["score_ready"], g + 1)
                for n in range(GT):
                    t = GT * g + n
                    gp.indirect_dma_start(out=regions, out_offset=bass.IndirectOffsetOnAxis(ap=pos[:, t:t + 1], axis=0),
                                          in_=rows[:, t, :], in_offset=None,
                                          bounds_check=PAD - 1, oob_is_err=False
                                          ).then_inc(s["early_scattered" if g < GA else "late_scattered"], 16)

            for st in range(STEPS):
                if 0 <= st - 2 < G:
                    rms(st - 2)
                if 0 <= st - 3 < G:
                    rstd2_of(st - 3)
                for m in STATS_AT.get(st, ()):
                    rstd1_of(m)
                if 0 <= st - 4 < G:
                    scatter(st - 4)
                if st == 2:
                    tile_numbers()

            def token_numbers(j, k, turn):
                pool.wait_ge(xs_loaded[k], turn * 16 + 16)
                if turn > 0:
                    pool.wait_ge(stored[k], turn * 16)
                gp.tensor_copy(tok[k][:, :], xs[k][:, C_ID:C_ID + 1].bitcast(I32)).then_inc(s["tok_ready"], 1)

            def store(j, k, turn):
                pool.wait_ge(s["ob_ready"], j + 1)
                pool.wait_ge(s["tok_ready"], j + 1)
                gp.indirect_dma_start(out=out_rows, out_offset=bass.IndirectOffsetOnAxis(ap=tok[k][:, 0:1], axis=0),
                                      in_=ob[k][:, :], in_offset=None,
                                      bounds_check=N - 1, oob_is_err=False).then_inc(stored[k], 16)

            token_numbers(0, 0, 0)
            for k in range(NB - 1):
                token_numbers(k + 1, k + 1, 0)
                store(k, k, 0)
            for j in range(NB, NT):
                token_numbers(j, j % NB, j // NB)
                store(j - 1, (j - 1) % NB, None)
            store(NT - 1, (NT - 1) % NB, None)
            for k in range(NB):
                pool.wait_ge(stored[k], 16 * len(range(k, NT, NB)))

        @block.scalar
        def _(act):
            ac = nc.scalar
            act.dma_start(dec_in[:, :], decay.rearrange("(p a) -> p a", a=1)).then_inc(s["decay_loaded"], 16)
            act.wait_ge(s["ident_step"], 1)
            ac.activation(warm[:, 0:1], ones_col[:, :], ACT.Exp)
            act.wait_ge(s["decay_loaded"], 16)
            ac.activation(dcol[:, 0:1], dec_in[:, :], ACT.Exp, scale=-1.0).then_inc(s["decay_exp"], 1)

            def normalise(g):
                act.wait_ge(s["shift1_ready"], load_of(g) + 1)
                if g >= 2:
                    act.wait_ge(s["xnT_ps_ready"], g - 1)
                for n in range(GT):
                    t = GT * g + n
                    last = ac.activation(xn[:, g % 2, n, :], x_all[:, t, :], ACT.Identity, bias=shift1[:, t:t + 1],
                                         scale=rstd1[:, t:t + 1])
                last.then_inc(s["xn_ready"], 1)

            normalise(0)
            act.wait_ge(s["wT_ps_ready"], 1)
            ac.copy(wT[:, 0:3, :], X_ps[:, 0:3 * D].rearrange("p (a b) -> p a b", a=3)).then_inc(s["wT_ready"], 1)

            def evac_xn(g):
                act.wait_ge(s["xnT_ps_ready"], g + 1)
                if g >= 2:
                    act.wait_ge(s["rkv_ready"], 3 * (g - 1))
                ac.copy(xnT[:, g % 2, :], T_ps[:, :]).then_inc(s["xnT_ready"], 1)

            def tanh_r(g):
                act.wait_ge(s["rkv_ready"], 3 * g + 3)
                if g >= 2:
                    act.wait_ge(s["y_ready"], g - 1)
                ac.activation(rt[:, g % 2, :], R_ps[:, :], ACT.Tanh, scale=0.5).then_inc(s["r_ready"], 1)

            def squares(g):
                act.wait_ge(s["y_ready"], g + 1)
                if g >= 2:
                    act.wait_ge(s["out_ready"], g - 1)
                ac.activation(y2[:, g % 2, :], y[:, g % 2, :], ACT.Square).then_inc(s["y2_ready"], 1)

            def evac_x1(g):
                act.wait_ge(s["x1T_ps_ready"], g + 1)
                if g >= 2:
                    act.wait_ge(s["logits_ready"], g - 1)
                ac.copy(x1T[:, g % 2, :], X_ps[:, :]).then_inc(s["x1T_ready"], 1)

            def exps(g):
                act.wait_ge(s["dl_ready"], g + 1)
                if g >= 2:
                    act.wait_ge(s["sx_ready"], g - 1)
                ac.activation(ex[:, g % 2, :, :], dl[:, g % 2, :, :], ACT.Exp).then_inc(s["ex_ready"], 1)

            evac_xn(0)
            normalise(1)
            for st in range(STEPS):
                if st < G:
                    tanh_r(st)
                if 0 <= st - 3 < G:
                    exps(st - 3)
                if 0 <= st - 2 < G:
                    evac_x1(st - 2)
                if st + 1 < G:
                    evac_xn(st + 1)
                if st < G:
                    squares(st)
                if st + 2 < G:
                    normalise(st + 2)
                if st == 0:
                    act.wait_ge(s["woT_ps_ready"], 1)
                    ac.activation(wT[:, 3, :], X_ps[:, 3 * D:4 * D], ACT.Copy, scale=lnw[:, 0:1]
                                  ).then_inc(s["woT_ready"], 1)

            ac.activation(warm[:, 1:2], ones_col[:, :], ACT.Gelu)
            act.wait_ge(s["b1T_ps_ready"], 1)
            ac.copy(biases[:, :].rearrange("p (e c) -> p e c", e=E)[:, :, 0:HC],
                    T_ps[:, 0:E * HC].rearrange("p (e c) -> p e c", e=E)).then_inc(s["b1T_ready"], 1)

            def evac_z(j, k, first):
                act.wait_ge(s["zT_ps_ready"], j + 1)
                if not first:
                    act.wait_ge(s["up_ready"], j - 1)
                ac.copy(znT[k % 2][:, :], zT_ps[k % 2][:, 0:P]).then_inc(s["zT_ready"], 1)

            def fetch_w1(j, k, off, first):
                if not first:
                    act.wait_ge(s["up_ready"], j - 1)
                ac.copy(w1_cur[k % 2][:, :], w1_sb[:, bass.ds(off, HID)]).then_inc(s["w1_ready"], 1)

            def gelu(j, k, first):
                act.wait_ge(s["hb_ready"], j + 1)
                if not first:
                    act.wait_ge(s["down_ready"], j - 1)
                ac.activation(hT[k % 2][:, :], hb[k % 2][:, :], ACT.Gelu).then_inc(s["hT_ready"], 1)

            act.wait_ge(s["tab_ready"], 1)
            act.wait_ge(s["ffn_loaded"], 16 * 4)
            off = table(act, tab_off, 0, 4, (E - 1) * HID)
            fetch_w1(0, 0, off[0], True)
            fetch_w1(1, 1, off[1], True)
            evac_z(0, 0, True)
            evac_z(1, 1, True)
            gelu(0, 0, True)
            fetch_w1(2, 2, off[2], False)
            evac_z(2, 2, False)
            gelu(1, 1, True)
            fetch_w1(3, 3, off[3], False)
            loops = (NT - 4) // LOOP_TILES
            with act.Fori(0, loops) as i:
                act.wait_ge(s["tab_ready"], i + 1)
                off = table(act, tab_off, i * LOOP_TILES + 4, LOOP_TILES, (E - 1) * HID)
                for k in range(LOOP_TILES):
                    j = i * LOOP_TILES + 2 + k
                    evac_z(j + 1, k + 3, False)
                    gelu(j, k + 2, False)
                    fetch_w1(j + 2, k + 4, off[k], False)
            last_tiles = loops * LOOP_TILES + 2
            off = table(act, tab_off, last_tiles + 2, NT - last_tiles - 2, (E - 1) * HID)
            for j in range(last_tiles, NT):
                if j + 1 < NT:
                    evac_z(j + 1, j + 1, False)
                gelu(j, j, False)
                if j + 2 < NT:
                    fetch_w1(j + 2, j + 2, off[j - last_tiles], False)

        @block.vector
        def _(dve):
            ve = nc.vector

            def stats1_of(m):
                t0, t1 = GT * X_LOADS[m][0], GT * X_LOADS[m][1]
                dve.wait_ge(x_loaded[m], 16)
                for n in range(t0, t1):
                    last = ve.bn_stats(st1[:, n, :], x_all[:, n, :])
                last.then_inc(s["st1_done"], 1)
                dve.wait_ge(s["st1_done"], m + 1)
                for n in range(t0, t1):
                    last = ve.bn_aggr(mv1[:, n, :], st1[:, n, :])
                last.then_inc(s["mv1_ready"], 1)
                dve.wait_ge(s["mv1_ready"], m + 1)
                ve.tensor_scalar(ve1[:, t0:t1], mv1[:, t0:t1, 1], LN_EPS, None, ALU.add).then_inc(s["ve1_ready"], 1)

            def shift1_of(m):
                t0, t1 = GT * X_LOADS[m][0], GT * X_LOADS[m][1]
                dve.wait_ge(s["rstd1_ready"], m + 1)
                ve.scalar_tensor_tensor(shift1[:, t0:t1], mv1[:, t0:t1, 0], -1.0, rstd1[:, t0:t1],
                                        ALU.mult, ALU.mult).then_inc(s["shift1_ready"], 1)

            def sigmoid():
                dve.wait_ge(s["decay_exp"], 1)
                ve.tensor_scalar(dcol[:, 1:2], dcol[:, 0:1], 1.0, None, ALU.add).then_inc(s["decay_step"], 1)
                dve.wait_ge(s["decay_step"], 1)
                ve.reciprocal(dcol[:, 0:1], dcol[:, 1:2]).then_inc(s["decay_step"], 1)
                dve.wait_ge(s["decay_step"], 2)
                ve.tensor_scalar(dcol[:, 2:3], dcol[:, 0:1], 1e-7, None, ALU.max).then_inc(s["decay_step"], 1)

            def decays():
                dve.wait_ge(s["decay_step"], 3)
                dve.wait_ge(s["scale_start"], 1)
                ve.tensor_scalar(dec_row[:, :], zero_row[:, :], dcol[:, 2:3], None, ALU.add
                                 ).then_inc(s["gain_step"], 1)
                dve.wait_ge(s["gain_step"], 1)
                ve.tensor_tensor_scan(scale_t[:, 1:T], dec_row[:, 1:T], zero_row[:, 1:T], 1.0, ALU.mult, ALU.add
                                      ).then_inc(s["gain_step"], 1)
                dve.wait_ge(s["gain_step"], 2)
                ve.tensor_scalar(gain[:, :], scale_t[:, :], 0.5e10, 0.5, ALU.mult, ALU.min)
                ve.memset(dec_row[:, 0:1], 0.0).then_inc(s["gain_ready"], 1)
                dve.wait_ge(s["gain_ready"], 1)

            def gate_squares():
                dve.wait_ge(s["params_loaded"], PARAMS)
                ve.tensor_tensor(gsq[:, :], wg_sb[:, :], wg_sb[:, :], ALU.mult).then_inc(s["gate_step"], 1)
                dve.wait_ge(s["gate_step"], 1)
                ve.tensor_reduce(gn[:, 0:1], gsq[:, :], AX.X, ALU.add).then_inc(s["gate_step"], 1)

            def gate_unit():
                dve.wait_ge(s["gate_norm"], 1)
                ve.tensor_scalar(gn[:, 2:3], gn[:, 1:2], GATE_EPS, None, ALU.max).then_inc(s["gate_step"], 1)
                dve.wait_ge(s["gate_step"], 3)
                ve.reciprocal(gn[:, 3:4], gn[:, 2:3]).then_inc(s["gate_step"], 1)
                dve.wait_ge(s["gate_step"], 4)
                ve.tensor_scalar(wgu[:, :], wg_sb[:, :], gn[:, 3:4], None, ALU.mult).then_inc(s["gate_step"], 1)

            def gate_turned():
                dve.wait_ge(s["gate_pe"], 1)
                ve.tensor_copy(wguT[:, :], L_ps[0:GD, 0:E]).then_inc(s["gate_step"], 1)

            def gate_reduced():
                dve.wait_ge(s["gate_pe"], 2)
                ve.tensor_copy(gate_m[:, :], L_ps[:, 0:E]).then_inc(s["gate_step"], 1)

            def gate_centred():
                dve.wait_ge(s["gate_pe"], 3)
                dve.wait_ge(s["gate_step"], 7)
                ve.tensor_tensor(gate_c[:, :], gate_m[:, :], L_ps[:, 0:E], ALU.subtract).then_inc(s["gate_step"], 1)

            def residual(g, n0, n1):
                for n in range(n0, n1):
                    t = GT * g + n
                    last = ve.scalar_tensor_tensor(rows[:, t, 0:D], O_ps[:, n * D:(n + 1) * D],
                                                   rrms[:, g % 2, n:n + 1], x_all[:, t, :], ALU.mult, ALU.add)
                return last

            def statistics(g, n0, n1):
                for n in range(n0, n1):
                    last = ve.bn_stats(st2[:, n, :], rows[:, GT * g + n, 0:D])
                return last

            def mean_square(g):
                dve.wait_ge(s["out_ready"], g + 1)
                ve.tensor_scalar(ssm[:, g % 2, :], S_ps[:, 0:GT], 1.0 / D, RMS_EPS, ALU.mult, ALU.add
                                 ).then_inc(s["ssm_ready"], 1)

            def step(st):
                rec, res, sta, cho = st - 1, st - 2, st - 3, st - 4
                c = rec % GPB * GC
                if 0 <= rec < G:
                    dve.wait_ge(s["rkv_ready"], 3 * rec + 1)
                    ve.tensor_tensor(vg[:, :], V_ps[:, :], gain[:, c:c + GC], ALU.mult).then_inc(s["vg_ready"], 1)
                if st == 2:
                    gate_turned()
                if 0 <= cho < G:
                    dve.wait_ge(s["logits_ready"], cho + 1)
                    dve.wait_ge(s["rstd2_ready"], cho + 1)
                    t0 = GT * cho
                    ve.tensor_tensor(lg[:, :, :], L_ps[:, 0:GT * E].rearrange("p (a b) -> p a b", a=GT),
                                     rows[:, t0:t0 + GT, C_RSTD:C_RSTD + 1].broadcast_to([P, GT, E]),
                                     ALU.mult).then_inc(s["lg_ready"], 1)
                if 0 <= rec < G:
                    dve.wait_ge(s["rkv_ready"], 3 * rec + 2)
                    dve.wait_ge(s["vg_ready"], rec + 1)
                    ve.tensor_tensor(kv[:, :], K_ps[:, :], vg[:, :], ALU.mult).then_inc(s["kv_ready"], 1)
                if 0 <= cho < G:
                    dve.wait_ge(s["lg_ready"], cho + 1)
                    ve.tensor_reduce(mx[:, :], lg[:, :, :], AX.X, ALU.max).then_inc(s["mx_ready"], 1)
                if 0 <= rec < G:
                    dve.wait_ge(s["kv_ready"], rec + 1)
                    ve.tensor_tensor_scan(state[:, rec % 2, :], dec_row[:, c:c + GC], kv[:, :],
                                          state[:, (rec + 1) % 2, GC - 1:GC], ALU.mult, ALU.add
                                          ).then_inc(s["state_ready"], 1)
                if 0 <= cho < G:
                    dve.wait_ge(s["mx_ready"], cho + 1)
                    if cho >= 2:
                        dve.wait_ge(s["ex_ready"], cho - 1)
                    ve.tensor_tensor(dl[:, cho % 2, :, :], lg[:, :, :], mx[:, :].unsqueeze(2).broadcast_to([P, GT, E]),
                                     ALU.subtract).then_inc(s["dl_ready"], 1)
                if 0 <= rec < G:
                    dve.wait_ge(s["state_ready"], rec + 1)
                    dve.wait_ge(s["r_ready"], rec + 1)
                    if rec >= 2:
                        dve.wait_ge(s["out_ready"], rec - 1)
                        dve.wait_ge(s["y2_ready"], rec - 1)
                    if st == 3:
                        gate_centred()
                    ve.scalar_tensor_tensor(y[:, rec % 2, :], rt[:, rec % 2, :], 1.0, state[:, rec % 2, :],
                                            ALU.add, ALU.mult).then_inc(s["y_ready"], 1)
                if st == 1:
                    gate_unit()
                if st == 2:
                    gate_reduced()
                for m in STATS_AT.get(st - 1, ()):
                    shift1_of(m)
                if 0 <= cho < G:
                    if cho == 0:
                        dve.wait_ge(s["consts_ready"], 1)
                    dve.wait_ge(s["dl_ready"], cho + 1)
                    ve.scalar_tensor_tensor(cand[:, :, :], dl[:, cho % 2, :, :], 0.0, first_w[:, :, :],
                                            ALU.is_equal, ALU.mult).then_inc(s["cand_ready"], 1)
                if 0 <= res < G - 1:
                    mean_square(res)
                if 0 <= sta < G:
                    statistics(sta, 0, 1)
                if 0 <= cho < G:
                    dve.wait_ge(s["cand_ready"], cho + 1)
                    ve.tensor_reduce(cmx[:, :], cand[:, :, :], AX.X, ALU.max).then_inc(s["cmx_ready"], 1)
                if 0 <= sta < G:
                    statistics(sta, 1, 2)
                if 0 <= cho < G:
                    dve.wait_ge(s["cmx_ready"], cho + 1)
                    if cho >= 2:
                        dve.wait_ge(s["rank_ready"], cho - 1)
                    ve.tensor_tensor(oneh[:, cho % 2, :, :], cand[:, :, :],
                                     cmx[:, :].unsqueeze(2).broadcast_to([P, GT, E]), ALU.is_equal
                                     ).then_inc(s["oneh_ready"], 1)
                if 0 <= sta < G:
                    statistics(sta, 2, GT).then_inc(s["st2_ready"], 1)
                if 0 <= cho < G:
                    dve.wait_ge(s["oneh_ready"], cho + 1)
                    with nc.allow_low_precision(reason="whole numbers up to GT"):
                        ve.tensor_reduce(group_n[:, cho, :], oneh[:, cho % 2, :, :].rearrange("p a b -> p b a"),
                                         AX.X, ALU.add).then_inc(s["group_n_ready"], 1)
                if 0 <= sta < G:
                    dve.wait_ge(s["st2_ready"], sta + 1)
                    for n in range(GT):
                        last = ve.bn_aggr(rows[:, GT * sta + n, C_MEAN:C_MEAN + 2], st2[:, n, :])
                    last.then_inc(s["mv2_ready"], 1)
                if 0 <= sta < G:
                    dve.wait_ge(s["mv2_ready"], sta + 1)
                    ve.tensor_scalar(ve2[:, sta % 2, :], rows[:, GT * sta:GT * sta + GT, C_VAR], LN_EPS, None, ALU.add
                                     ).then_inc(s["ve2_ready"], 1)
                if 0 <= cho < G:
                    dve.wait_ge(s["ex_ready"], cho + 1)
                    ve.tensor_reduce(sx[:, cho % 2, :], ex[:, cho % 2, :, :], AX.X, ALU.add).then_inc(s["sx_ready"], 1)
                if res == G - 1:
                    mean_square(res)
                if 0 <= res < G:
                    dve.wait_ge(s["rrms_ready"], res + 1)
                    residual(res, 0, 1)
                if 0 <= cho < G:
                    dve.wait_ge(s["rank_ready"], cho + 1)
                    ve.tensor_tensor(pos_m[:, :, :], rank_ps.rearrange("p (a b) -> p a b", a=GT),
                                     oneh[:, cho % 2, :, :], ALU.mult).then_inc(s["posm_ready"], 1)
                    dve.wait_ge(s["sx_ready"], cho + 1)
                    ve.reciprocal(rows[:, GT * cho:GT * cho + GT, C_SCORE], sx[:, cho % 2, :]
                                  ).then_inc(s["score_ready"], 1)
                if 0 <= res < G:
                    residual(res, 1, 2)
                if 0 <= cho < G:
                    dve.wait_ge(s["posm_ready"], cho + 1)
                    with nc.allow_low_precision(reason="whole numbers"):
                        ve.tensor_reduce(pos[:, GT * cho:GT * cho + GT], pos_m[:, :, :], AX.X, ALU.add
                                         ).then_inc(s["pos_ready"], 1)
                if 0 <= res < G:
                    residual(res, 2, GT).then_inc(s["x1_ready"], 1)
                for m in STATS_AT.get(st, ()):
                    stats1_of(m)

            stats1_of(0)
            stats1_of(1)
            shift1_of(0)
            sigmoid()
            decays()
            shift1_of(1)
            ve.memset(state[:, 1, GC - 1:GC], 0.0)
            gate_squares()
            stats1_of(2)

            def place_tiles(j0, j1, step, taken_0):
                n = j1 - j0
                dve.wait_ge(s["tab_step"], step)
                ve.tensor_tensor_scan(tl_end[:, :], ones_row[:, :], tl[:, :], 0.0, ALU.mult, ALU.add
                                      ).then_inc(s["tab_step"], 1)
                dve.wait_ge(s["tab_step"], step + 1)
                ve.tensor_tensor(past[:, 0:n, :], j_f[:, 0:n, :], tl_end[:, :].unsqueeze(1).broadcast_to([1, n, E]),
                                 ALU.is_ge).then_inc(s["tab_step"], 1)
                dve.wait_ge(s["tab_step"], step + 2)
                ve.tensor_tensor(past_t[:, 0:n, :], past[:, 0:n, :],
                                 weight[:, :].unsqueeze(1).broadcast_to([1, n, E]), ALU.mult)
                ve.tensor_reduce(exp_j[:, 0:n], past[:, 0:n, :], AX.X, ALU.add).then_inc(s["tab_step"], 1)
                dve.wait_ge(s["tab_step"], step + 3)
                ve.tensor_reduce(skip_j[:, 0:n], past_t[:, 0:n, :], AX.X, ALU.add)
                ve.tensor_scalar(row_b[:, 0:n], exp_j[:, 0:n], float(REG), None, ALU.mult).then_inc(s["tab_step"], 1)
                dve.wait_ge(s["tab_step"], step + 4)
                ve.scalar_tensor_tensor(row_a[:, 0:n], j_f[:, 0:n, 0], taken_0, skip_j[:, 0:n],
                                        ALU.add, ALU.subtract).then_inc(s["tab_step"], 1)
                dve.wait_ge(s["tab_step"], step + 5)
                ve.scalar_tensor_tensor(row_b[:, 0:n], row_a[:, 0:n], float(P), row_b[:, 0:n], ALU.mult, ALU.add
                                        ).then_inc(s["tab_step"], 1)
                dve.wait_ge(s["tab_step"], step + 6)
                with nc.allow_low_precision(reason="whole numbers"):
                    ve.tensor_scalar(tab_off[:, j0:j1], exp_j[:, 0:n], float(E - 1), float(HID), ALU.min, ALU.mult)
                    ve.tensor_scalar(tab_bias[:, j0:j1], exp_j[:, 0:n], float(E - 1), float(BIAS), ALU.min, ALU.mult)
                    return ve.tensor_scalar(tab_row[:, j0:j1], row_b[:, 0:n], float(PAD), None, ALU.min)

            P_BITS = P.bit_length() - 1

            def place_early_tiles():
                dve.wait_ge(s["counts_ready"], 1)
                dve.wait_ge(s["numbers_ready"], 1)
                ve.memset(taken[:, E:E + 1], 0.0)
                with nc.allow_low_precision(reason="whole numbers"):
                    ve.tensor_copy(cnt_i[0:1, 0, :], K_ps[0:1, 0:E]).then_inc(s["tab_step"], 1)
                    dve.wait_ge(s["tab_step"], 1)
                    ve.tensor_scalar(cnt_i[0:1, 1, :], cnt_i[0:1, 0, :], P_BITS, None, ALU.arith_shift_right
                                     ).then_inc(s["tab_step"], 1)
                dve.wait_ge(s["tab_step"], 2)
                ve.tensor_copy(tl[:, :], cnt_i[0:1, 1, :])
                ve.tensor_copy(weight[:, :], cnt_i[0:1, 1, :]).then_inc(s["tab_step"], 1)
                place_tiles(0, NA, 3, 0.0).then_inc(s["tab_ready"], 1)

            def take_counts():
                dve.wait_ge(s["counts_ready"], 2)
                with nc.allow_low_precision(reason="whole numbers"):
                    ve.tensor_tensor(fill_row[:, :], K_ps[0:1, 0:E], reg_base[:, :], ALU.add
                                     ).then_inc(s["fill_ready"], 1)
                    ve.tensor_scalar(cnt_i[0:1, 0, :], K_ps[0:1, 0:E], float(P - 1), None, ALU.add
                                     ).then_inc(s["tab_step"], 1)
                ve.scalar_tensor_tensor(room[:, 0, :], tl[:, :], float(NA), tl_end[:, :], ALU.add, ALU.subtract
                                        ).then_inc(s["tab_step"], 1)
                dve.wait_ge(s["tab_step"], 11)
                with nc.allow_low_precision(reason="whole numbers"):
                    ve.tensor_scalar(cnt_i[0:1, 1, :], cnt_i[0:1, 0, :], P_BITS, None, ALU.arith_shift_right
                                     ).then_inc(s["tab_step"], 1)
                ve.scalar_tensor_tensor(taken[:, 0:E], room[:, 0, :], 0.0, tl[:, :], ALU.max, ALU.min
                                        ).then_inc(s["tab_step"], 1)

            def place_late_tiles():
                dve.wait_ge(s["tab_step"], 13)
                ve.tensor_tensor(tl[:, :], cnt_i[0:1, 1, :], taken[:, 0:E], ALU.subtract)
                ve.tensor_tensor(weight[:, :], cnt_i[0:1, 1, :], taken[:, 1:E + 1], ALU.subtract
                                 ).then_inc(s["tab_step"], 1)
                place_tiles(NA, NT, 14, taken[:, 0:1]).then_inc(s["tab_ready"], NT // LOOP_TILES)

            for st in range(1, STEPS):
                step(st)
                if st == GA + 4:
                    place_early_tiles()
            take_counts()

            def norm_z(j, k, turn, first):
                dve.wait_ge(xs_loaded[k], turn * 16 + 16)
                if not first:
                    dve.wait_ge(s["zT_ps_ready"], j - 1)
                ve.tensor_scalar(zn[k % 2][:, :], xs[k][:, 0:D], xs[k][:, C_MEAN:C_MEAN + 1],
                                 xs[k][:, C_RSTD:C_RSTD + 1], ALU.subtract, ALU.mult).then_inc(s["zn_ready"], 1)

            def add_b1(j, k, at, first):
                dve.wait_ge(s["up_ready"], j + 1)
                if not first:
                    dve.wait_ge(s["hT_ready"], j - 1)
                ve.tensor_tensor(hb[k % 2][:, :].rearrange("p (c t) -> p c t", c=HC),
                                 up_ps[k % 2][:, :].rearrange("p (c t) -> p c t", c=HC),
                                 biases[:, bass.ds(at, HC)].unsqueeze(2).broadcast_to([P, HC, P]), ALU.add
                                 ).then_inc(s["hb_ready"], 1)

            def finish(j, k, at, turn, first):
                dve.wait_ge(s["down_ready"], j + 1)
                ve.tensor_tensor(yb[k % 2][:, :], dn_ps[k % 2][:, 0:D], biases[:, bass.ds(at + HC, D)], ALU.add
                                 ).then_inc(s["yb_ready"], 1)
                dve.wait_ge(s["yb_ready"], j + 1)
                if not first:
                    dve.wait_ge(stored[k], turn * 16)
                ve.scalar_tensor_tensor(ob[k][:, :], yb[k % 2][:, :], xs[k][:, C_SCORE:C_SCORE + 1],
                                        xs[k][:, 0:D], ALU.mult, ALU.add).then_inc(s["ob_ready"], 1)

            dve.wait_ge(s["b1T_ready"], 1)
            dve.wait_ge(s["tab_ready"], 1)
            dve.wait_ge(s["ffn_loaded"], 16 * 4)
            norm_z(0, 0, 0, True)
            norm_z(1, 1, 0, True)
            place_late_tiles()
            at = table(dve, tab_bias, 0, NB + 1, (E - 1) * BIAS)
            for j in range(NB + 1):
                add_b1(j, j, at[j], j < 2)
                norm_z(j + 2, (j + 2) % NB, (j + 2) // NB, False)
                if j >= 1:
                    finish(j - 1, j - 1, at[j - 1], 0, True)
            dve.wait_ge(s["tab_ready"], 2)
            loops = (NT - 3 - NB) // LOOP_TILES
            with dve.Fori(0, loops) as i:
                at = table(dve, tab_bias, i * LOOP_TILES + NB, LOOP_TILES + 1, (E - 1) * BIAS)
                for k in range(LOOP_TILES):
                    j = i * LOOP_TILES + NB + 1 + k
                    add_b1(j, 1 + k, at[k + 1], False)
                    norm_z(j + 2, (3 + k) % NB, i + 1 + (3 + k) // NB, False)
                    finish(j - 1, k, at[k], i + 1, False)
            last_tiles = loops * LOOP_TILES + NB + 1
            at = table(dve, tab_bias, last_tiles - 1, NT - last_tiles + 1, (E - 1) * BIAS)
            for j in range(last_tiles, NT):
                add_b1(j, j, at[j - last_tiles + 1], False)
                if j + 2 < NT:
                    norm_z(j + 2, (j + 2) % NB, (j + 2) // NB, False)
                finish(j - 1, (j - 1) % NB, at[j - last_tiles], (j - 1) // NB, False)
            finish(NT - 1, (NT - 1) % NB, at[NT - last_tiles], (NT - 1) // NB, False)

        @block.tensor
        def _(pe):
            te = nc.tensor

            def keep_busy(n):
                for _ in range(n):
                    te.matmul(L_ps[:, :].rearrange("p (a b) -> p a b", a=GT), ones_bf[:, :],
                              ones_bf[:, :].unsqueeze(1).broadcast_to([P, GT, P]), start=True, stop=True)

            pe.wait_ge(s["ident_ready"], 1)
            keep_busy(8)
            pe.wait_ge(s["mats_loaded"], 16 * 3)
            for n in range(3):
                last = te.transpose(X_ps[:, n * D:(n + 1) * D], w_nat[:, n, :], ident[:, :])
            last.then_inc(s["wT_ps_ready"], 1)

            keep_busy(4)

            def turn_wo():
                pe.wait_ge(s["wo_loaded"], 16 * 2)
                pe.wait_ge(s["wT_ready"], 1)
                te.transpose(X_ps[:, 3 * D:4 * D], w_nat[:, 3, :], ident[:, :]).then_inc(s["woT_ps_ready"], 1)

            def gate_turned():
                pe.wait_ge(s["gate_step"], 5)
                te.transpose(L_ps[0:GD, 0:E], wgu[:, :], ident[0:E, 0:E]).then_inc(s["gate_pe"], 1)

            def gate_reduced():
                pe.wait_ge(s["gate_step"], 6)
                pe.wait_ge(s["params_loaded"], PARAMS)
                te.matmul(L_ps[:, 0:E], wgr[:, :], wguT[:, :], start=True, stop=True).then_inc(s["gate_pe"], 1)

            def gate_mean():
                pe.wait_ge(s["gate_step"], 7)
                te.matmul(L_ps[:, 0:E], mean_w[:, :], gate_m[:, :], start=True, stop=True).then_inc(s["gate_pe"], 1)

            def project_out(g):
                pe.wait_ge(s["y_ready"], g + 1)
                pe.wait_ge(s["y2_ready"], g + 1)
                if g >= 1:
                    pe.wait_ge(s["x1_ready"], g)
                if g >= 3:
                    pe.wait_ge(s["posm_ready"], g - 2)
                for n in range(GT):
                    te.matmul(S_ps[:, n:n + 1], y2[:, g % 2, n * P:(n + 1) * P], ones_col[:, :], start=True, stop=True)
                for n in range(GT):
                    last = te.matmul(O_ps[:, n * D:(n + 1) * D], y[:, g % 2, n * P:(n + 1) * P], wT[:, 3, :],
                                     start=True, stop=True)
                last.then_inc(s["out_ready"], 1)

            def turn_xn(g):
                pe.wait_ge(s["xn_ready"], g + 1)
                if g >= 1:
                    pe.wait_ge(s["xnT_ready"], g)
                for n in range(GT):
                    last = te.transpose(T_ps[:, n * P:(n + 1) * P], xn[:, g % 2, n, :], ident[:, :])
                last.then_inc(s["xnT_ps_ready"], 1)

            def project_in(g):
                pe.wait_ge(s["xnT_ready"], g + 1)
                if g >= 1:
                    pe.wait_ge(s["vg_ready"], g)
                te.matmul(V_ps[:, :], wT[:, 2, :], xnT[:, g % 2, :], start=True, stop=True
                          ).then_inc(s["rkv_ready"], 1)
                if g >= 1:
                    pe.wait_ge(s["kv_ready"], g)
                te.matmul(K_ps[:, :], wT[:, 1, :], xnT[:, g % 2, :], start=True, stop=True
                          ).then_inc(s["rkv_ready"], 1)
                if g >= 1:
                    pe.wait_ge(s["r_ready"], g)
                te.matmul(R_ps[:, :], wT[:, 0, :], xnT[:, g % 2, :], start=True, stop=True
                          ).then_inc(s["rkv_ready"], 1)

            def turn_x1(g):
                pe.wait_ge(s["x1_ready"], g + 1)
                if g >= 1:
                    pe.wait_ge(s["x1T_ready"], g)
                for n in range(GT):
                    last = te.transpose(X_ps[:, n * P:(n + 1) * P], rows[:, GT * g + n, 0:D], ident[:, :])
                last.then_inc(s["x1T_ps_ready"], 1)

            def ranks(g):
                pe.wait_ge(s["oneh_ready"], g + 1)
                if g >= 1:
                    pe.wait_ge(s["group_n_ready"], g)
                pe.wait_ge(s["ssm_ready"], min(g + 3, G))
                of_tiles = rank_ps.rearrange("p (a b) -> p a b", a=GT)
                te.matmul(rank_ps, before[:, :], oneh[:, g % 2, :, :].rearrange("p a b -> p (a b)"),
                          start=True, stop=False)
                te.matmul(of_tiles, ones_bf[0:1, :], reg_part[:, :, :], start=False, stop=False)
                for m in range(g):
                    te.matmul(of_tiles, ones_bf[:, :], group_n[:, m, :].unsqueeze(1).broadcast_to([P, GT, E]),
                              start=False, stop=False)
                for n in range(GT - 1):
                    last = te.matmul(of_tiles[:, n + 1:GT, :], ones_bf[:, :],
                                     oneh[:, g % 2, n, :].unsqueeze(1).broadcast_to([P, GT - 1 - n, E]),
                                     start=False, stop=(n == GT - 2))
                last.then_inc(s["rank_ready"], 1)

            def logits(g):
                pe.wait_ge(s["x1T_ready"], g + 1)
                if g >= 1:
                    pe.wait_ge(s["lg_ready"], g)
                for n in range(GT):
                    last = te.matmul(L_ps[:, n * E:(n + 1) * E], x1T[:, g % 2, n * P:(n + 1) * P], gate_c[:, :],
                                     start=True, stop=True)
                last.then_inc(s["logits_ready"], 1)

            def expert_counts(g):
                pe.wait_ge(s["group_n_ready"], g)
                for m in range(g):
                    last = te.matmul(K_ps[:, 0:E], ones_bf[:, :], group_n[:, m, :], start=(m == 0), stop=(m == g - 1))
                last.then_inc(s["counts_ready"], 1)

            turn_xn(0)
            keep_busy(2)
            for st in range(STEPS):
                if st == GA + 4:
                    expert_counts(GA)
                if 0 <= st - 4 < G:
                    ranks(st - 4)
                if 0 <= st - 3 < G:
                    if st == 3:
                        pe.wait_ge(s["gate_step"], 8)
                    logits(st - 3)
                if st < G:
                    if st == 0:
                        pe.wait_ge(s["wT_ready"], 1)
                    project_in(st)
                if st == 0:
                    turn_wo()
                if st == 1:
                    gate_turned()
                if st == 2:
                    gate_mean()
                if 0 <= st - 1 < G:
                    if st == 1:
                        pe.wait_ge(s["woT_ready"], 1)
                    project_out(st - 1)
                if st == 1:
                    gate_reduced()
                if 0 <= st - 2 < G:
                    turn_x1(st - 2)
                if st + 1 < G:
                    turn_xn(st + 1)
            pe.wait_ge(s["ffn_loaded"], 16 * 4)
            pe.wait_ge(s["xnT_ready"], G)
            te.transpose(T_ps[:, 0:E * HC], b1_nat[:, :], ident[0:E * HC, 0:E * HC]).then_inc(s["b1T_ps_ready"], 1)
            expert_counts(G)

            pe.wait_ge(s["tab_ready"], 1)
            pe.wait_ge(s["early_scattered"], 16 * GT * GA)
            keep_busy(2)
            pe.wait_ge(s["b1T_ready"], 1)

            def turn_z(j, k):
                pe.wait_ge(s["zn_ready"], j + 1)
                te.transpose(zT_ps[k % 2][:, 0:P], zn[k % 2][:, :], ident[:, :]).then_inc(s["zT_ps_ready"], 1)

            def up(j, k, first):
                pe.wait_ge(s["zT_ready"], j + 1)
                pe.wait_ge(s["w1_ready"], j + 1)
                if not first:
                    pe.wait_ge(s["hb_ready"], j - 1)
                for c in range(HC):
                    last = te.matmul(up_ps[k % 2][:, c * P:(c + 1) * P], w1_cur[k % 2][:, c * P:(c + 1) * P],
                                     znT[k % 2][:, :], start=True, stop=True)
                last.then_inc(s["up_ready"], 1)

            def down(j, k, off, first):
                pe.wait_ge(s["hT_ready"], j + 1)
                if not first:
                    pe.wait_ge(s["yb_ready"], j - 1)
                for c in range(HC):
                    last = te.matmul(dn_ps[k % 2][:, 0:D], hT[k % 2][:, c * P:(c + 1) * P],
                                     w2_sb[:, bass.ds(off + c * D, D)], start=(c == 0), stop=(c == HC - 1))
                last.then_inc(s["down_ready"], 1)

            off = table(pe, tab_off, 0, 2, (E - 1) * HID)
            turn_z(0, 0)
            turn_z(1, 1)
            up(0, 0, True)
            for j in range(1, 3):
                up(j, j, j < 2)
                turn_z(j + 1, j + 1)
                down(j - 1, j - 1, off[j - 1], True)
            loops = (NT - 4) // LOOP_TILES
            with pe.Fori(0, loops) as i:
                pe.wait_ge(s["tab_ready"], i + 1)
                off = table(pe, tab_off, i * LOOP_TILES + 2, LOOP_TILES, (E - 1) * HID)
                for k in range(LOOP_TILES):
                    j = i * LOOP_TILES + 3 + k
                    up(j, 3 + k, False)
                    turn_z(j + 1, 3 + k + 1)
                    down(j - 1, 3 + k - 1, off[k], False)
            last_tiles = loops * LOOP_TILES + 3
            off = table(pe, tab_off, last_tiles - 1, NT + 1 - last_tiles, (E - 1) * HID)
            for j in range(last_tiles, NT + 1):
                if j < NT:
                    up(j, j, False)
                if j + 1 < NT:
                    turn_z(j + 1, j + 1)
                down(j - 1, j - 1, off[j - last_tiles], False)


_INS = ['L0_attn_x', 'L0_attn_Wr', 'L0_attn_Wk', 'L0_attn_Wv', 'L0_attn_Wo', 'L0_attn_decay', 'L0_attn_ln_w',
        'L0_ffn_wg_red', 'L0_ffn_wg', 'L0_ffn_w1', 'L0_ffn_b1', 'L0_ffn_w2', 'L0_ffn_b2']


def kernel(**inputs):
    import numpy as _np
    import concourse.bacc as _bacc
    from concourse import mybir as _mybir
    from concourse.bass_utils import run_bass_kernel_spmd as _run

    nc = _bacc.Bacc("TRN2", target_bir_lowering=False, num_devices=1)
    arrays, args = {}, []
    for name in _INS:
        a = _np.ascontiguousarray(inputs[name])
        arrays[f"in_{name}_dram"] = a
        args.append(nc.dram_tensor(f"in_{name}_dram", a.shape, _mybir.dt.from_np(a.dtype), kind="ExternalInput").ap())
    shape = inputs['L0_attn_x'].shape
    args.append(nc.dram_tensor("out_0_dram", shape, _mybir.dt.float32, kind="ExternalOutput").ap())
    rwkv_moe_layer(nc, *args)
    r = _run(nc, [arrays], core_ids=[0])
    return r.results[0]["out_0_dram"]
```
